# Optimizing a Trainium2 kernel written in Bass

```python
import numpy as np
import jax
import jax.numpy as jnp

def _softmax(x, axis=-1):
    return jax.nn.softmax(x, axis=axis)

def _gelu(x):
    return jax.nn.gelu(x, approximate=True)

def _silu(x):
    return jax.nn.silu(x)

def _sigmoid(x):
    return jax.nn.sigmoid(x)

def _layernorm(x, axis=-1, eps=1e-05):
    m = jnp.mean(x, axis=axis, keepdims=True)
    v = jnp.var(x, axis=axis, keepdims=True)
    return (x - m) / jnp.sqrt(v + eps)

def _scatter_add(tgt, idx, src, axis=0):
    return tgt.at[idx].add(src)

def _segment_sum(src, seg, n):
    return jax.ops.segment_sum(src, seg, n)
kernel_name = 'mk_rec_standalone_d1_rec_r8_7a23cd'

def setup_inputs(seed: int=0):
    np.random.seed(seed)
    _w = jnp.asarray

    def _rec_inputs():
        import jax
        import jax.numpy as jnp
        _rk = jax.random.key(seed)
        r_dense_inputs = -0.000692196 + 0.998807 * jax.random.normal(jax.random.fold_in(_rk, 1), (2048, 13), jnp.float32)
        r_sparse_inputs = jnp.stack([jax.random.randint(jax.random.fold_in(jax.random.fold_in(_rk, 2), 0), (2048,), 0, 99999, jnp.int32), jax.random.randint(jax.random.fold_in(jax.random.fold_in(_rk, 2), 1), (2048,), 0, 12499, jnp.int32), jax.random.randint(jax.random.fold_in(jax.random.fold_in(_rk, 2), 2), (2048,), 4, 99997, jnp.int32), jax.random.randint(jax.random.fold_in(jax.random.fold_in(_rk, 2), 3), (2048,), 2, 99997, jnp.int32), jax.random.randint(jax.random.fold_in(jax.random.fold_in(_rk, 2), 4), (2048,), 1, 99988, jnp.int32), jax.random.randint(jax.random.fold_in(jax.random.fold_in(_rk, 2), 5), (2048,), 1, 99996, jnp.int32), jax.random.randint(jax.random.fold_in(jax.random.fold_in(_rk, 2), 6), (2048,), 12, 99997, jnp.int32), jax.random.randint(jax.random.fold_in(jax.random.fold_in(_rk, 2), 7), (2048,), 17, 99995, jnp.int32), jax.random.randint(jax.random.fold_in(jax.random.fold_in(_rk, 2), 8), (2048,), 0, 99998, jnp.int32), jax.random.randint(jax.random.fold_in(jax.random.fold_in(_rk, 2), 9), (2048,), 0, 99998, jnp.int32), jax.random.randint(jax.random.fold_in(jax.random.fold_in(_rk, 2), 10), (2048,), 3, 99993, jnp.int32), jax.random.randint(jax.random.fold_in(jax.random.fold_in(_rk, 2), 11), (2048,), 0, 99993, jnp.int32), jax.random.randint(jax.random.fold_in(jax.random.fold_in(_rk, 2), 12), (2048,), 1, 99988, jnp.int32), jax.random.randint(jax.random.fold_in(jax.random.fold_in(_rk, 2), 13), (2048,), 0, 99997, jnp.int32), jax.random.randint(jax.random.fold_in(jax.random.fold_in(_rk, 2), 14), (2048,), 3, 99993, jnp.int32), jax.random.randint(jax.random.fold_in(jax.random.fold_in(_rk, 2), 15), (2048,), 10, 99994, jnp.int32), jax.random.randint(jax.random.fold_in(jax.random.fold_in(_rk, 2), 16), (2048,), 10, 99998, jnp.int32), jax.random.randint(jax.random.fold_in(jax.random.fold_in(_rk, 2), 17), (2048,), 18, 99979, jnp.int32), jax.random.randint(jax.random.fold_in(jax.random.fold_in(_rk, 2), 18), (2048,), 1, 99996, jnp.int32), jax.random.randint(jax.random.fold_in(jax.random.fold_in(_rk, 2), 19), (2048,), 6, 99987, jnp.int32), jax.random.randint(jax.random.fold_in(jax.random.fold_in(_rk, 2), 20), (2048,), 6, 12500, jnp.int32), jax.random.randint(jax.random.fold_in(jax.random.fold_in(_rk, 2), 21), (2048,), 2, 12500, jnp.int32), jax.random.randint(jax.random.fold_in(jax.random.fold_in(_rk, 2), 22), (2048,), 7, 12498, jnp.int32), jax.random.randint(jax.random.fold_in(jax.random.fold_in(_rk, 2), 23), (2048,), 2, 99999, jnp.int32), jax.random.randint(jax.random.fold_in(jax.random.fold_in(_rk, 2), 24), (2048,), 29, 99990, jnp.int32), jax.random.randint(jax.random.fold_in(jax.random.fold_in(_rk, 2), 25), (2048,), 10, 99986, jnp.int32)], axis=1)
        return (r_dense_inputs, r_sparse_inputs)
    r_dense_inputs, r_sparse_inputs = _rec_inputs()

    def _L0_rec_setup():
        import jax, jax.numpy as jnp
        import numpy as np
        B = 2048
        DENSE = 13
        NF = 26
        D = 64
        VOCAB = 12500
        BOT = [512, 256, 64]
        TOP = [512, 256, 1]
        EPS = 1e-05

        def _bn(x, g, b):
            m = x.mean(axis=0)
            v = x.var(axis=0)
            return g * (x - m) * jax.lax.rsqrt(v + EPS) + b

        def _forward(sparse_inputs, dense_inputs, emb_tables, bot, top):
            x = dense_inputs
            for W, b, g, be in bot:
                x = _bn(jax.nn.relu(x @ W + b), g, be)
            embs = jax.vmap(lambda tbl, idx: tbl[idx], in_axes=(0, 1), out_axes=1)(emb_tables, sparse_inputs)
            T = jnp.concatenate([embs, x[:, None, :]], axis=1)
            Z = jnp.einsum('bnd,bmd->bnm', T, T)
            iu, ju = np.triu_indices(NF + 1, k=1)
            Zflat = Z[:, iu, ju]
            R = jnp.concatenate([x, Zflat], axis=1)
            h = R
            for W, b, g, be in top:
                h = _bn(jax.nn.relu(h @ W + b), g, be)
            return jax.nn.sigmoid(h)
        key = jax.random.key(seed)
        ks = iter(jax.random.split(key, 32))
        inp = {}
        inp['sparse_inputs'] = jax.random.randint(next(ks), (B, NF), 0, VOCAB)
        inp['dense_inputs'] = jax.random.normal(next(ks), (B, DENSE), dtype=jnp.float32)
        inp['emb_tables'] = jax.random.normal(next(ks), (NF, VOCAB, D), dtype=jnp.float32) * 0.01
        dims = [DENSE] + BOT
        for i in range(3):
            inp['bot_W%d' % i] = jax.random.normal(next(ks), (dims[i], dims[i + 1]), dtype=jnp.float32) * 0.05
            inp['bot_b%d' % i] = jnp.zeros((dims[i + 1],), jnp.float32)
            inp['bot_g%d' % i] = jnp.ones((dims[i + 1],), jnp.float32)
            inp['bot_beta%d' % i] = jnp.zeros((dims[i + 1],), jnp.float32)
        top_in = NF * (NF + 1) // 2 + D
        dims = [top_in] + TOP
        for i in range(3):
            inp['top_W%d' % i] = jax.random.normal(next(ks), (dims[i], dims[i + 1]), dtype=jnp.float32) * 0.05
            inp['top_b%d' % i] = jnp.zeros((dims[i + 1],), jnp.float32)
            inp['top_g%d' % i] = jnp.ones((dims[i + 1],), jnp.float32)
            inp['top_beta%d' % i] = jnp.zeros((dims[i + 1],), jnp.float32)
        return inp
    _L0_rec_all = _L0_rec_setup()
    _L0_rec_in = {k: v for k, v in _L0_rec_all.items() if k in ('emb_tables', 'bot_W0', 'bot_b0', 'bot_g0', 'bot_beta0', 'bot_W1', 'bot_b1', 'bot_g1', 'bot_beta1', 'bot_W2', 'bot_b2', 'bot_g2', 'bot_beta2', 'top_W0', 'top_b0', 'top_g0', 'top_beta0', 'top_W1', 'top_b1', 'top_g1', 'top_beta1', 'top_W2', 'top_b2', 'top_g2', 'top_beta2')}
    del _L0_rec_all
    return {'r_dense_inputs': r_dense_inputs, 'r_sparse_inputs': r_sparse_inputs, 'L0_rec_emb_tables': _L0_rec_in['emb_tables'], 'L0_rec_bot_W0': _L0_rec_in['bot_W0'], 'L0_rec_bot_b0': _L0_rec_in['bot_b0'], 'L0_rec_bot_g0': _L0_rec_in['bot_g0'], 'L0_rec_bot_beta0': _L0_rec_in['bot_beta0'], 'L0_rec_bot_W1': _L0_rec_in['bot_W1'], 'L0_rec_bot_b1': _L0_rec_in['bot_b1'], 'L0_rec_bot_g1': _L0_rec_in['bot_g1'], 'L0_rec_bot_beta1': _L0_rec_in['bot_beta1'], 'L0_rec_bot_W2': _L0_rec_in['bot_W2'], 'L0_rec_bot_b2': _L0_rec_in['bot_b2'], 'L0_rec_bot_g2': _L0_rec_in['bot_g2'], 'L0_rec_bot_beta2': _L0_rec_in['bot_beta2'], 'L0_rec_top_W0': _L0_rec_in['top_W0'], 'L0_rec_top_b0': _L0_rec_in['top_b0'], 'L0_rec_top_g0': _L0_rec_in['top_g0'], 'L0_rec_top_beta0': _L0_rec_in['top_beta0'], 'L0_rec_top_W1': _L0_rec_in['top_W1'], 'L0_rec_top_b1': _L0_rec_in['top_b1'], 'L0_rec_top_g1': _L0_rec_in['top_g1'], 'L0_rec_top_beta1': _L0_rec_in['top_beta1'], 'L0_rec_top_W2': _L0_rec_in['top_W2'], 'L0_rec_top_b2': _L0_rec_in['top_b2'], 'L0_rec_top_g2': _L0_rec_in['top_g2'], 'L0_rec_top_beta2': _L0_rec_in['top_beta2']}

def reference(r_dense_inputs, r_sparse_inputs, L0_rec_emb_tables, L0_rec_bot_W0, L0_rec_bot_b0, L0_rec_bot_g0, L0_rec_bot_beta0, L0_rec_bot_W1, L0_rec_bot_b1, L0_rec_bot_g1, L0_rec_bot_beta1, L0_rec_bot_W2, L0_rec_bot_b2, L0_rec_bot_g2, L0_rec_bot_beta2, L0_rec_top_W0, L0_rec_top_b0, L0_rec_top_g0, L0_rec_top_beta0, L0_rec_top_W1, L0_rec_top_b1, L0_rec_top_g1, L0_rec_top_beta1, L0_rec_top_W2, L0_rec_top_b2, L0_rec_top_g2, L0_rec_top_beta2):
    import jax
    import jax.numpy as jnp

    def _L0_rec_ref(sparse_inputs, dense_inputs, emb_tables, bot_W0, bot_b0, bot_g0, bot_beta0, bot_W1, bot_b1, bot_g1, bot_beta1, bot_W2, bot_b2, bot_g2, bot_beta2, top_W0, top_b0, top_g0, top_beta0, top_W1, top_b1, top_g1, top_beta1, top_W2, top_b2, top_g2, top_beta2):
        import jax, jax.numpy as jnp
        import numpy as np
        B = 2048
        DENSE = 13
        NF = 26
        D = 64
        VOCAB = 12500
        BOT = [512, 256, 64]
        TOP = [512, 256, 1]
        EPS = 1e-05

        def _bn(x, g, b):
            m = x.mean(axis=0)
            v = x.var(axis=0)
            return g * (x - m) * jax.lax.rsqrt(v + EPS) + b

        def _forward(sparse_inputs, dense_inputs, emb_tables, bot, top):
            x = dense_inputs
            for W, b, g, be in bot:
                x = _bn(jax.nn.relu(x @ W + b), g, be)
            embs = jax.vmap(lambda tbl, idx: tbl[idx], in_axes=(0, 1), out_axes=1)(emb_tables, sparse_inputs)
            T = jnp.concatenate([embs, x[:, None, :]], axis=1)
            Z = jnp.einsum('bnd,bmd->bnm', T, T)
            iu, ju = np.triu_indices(NF + 1, k=1)
            Zflat = Z[:, iu, ju]
            R = jnp.concatenate([x, Zflat], axis=1)
            h = R
            for W, b, g, be in top:
                h = _bn(jax.nn.relu(h @ W + b), g, be)
            return jax.nn.sigmoid(h)
        bot = [(bot_W0, bot_b0, bot_g0, bot_beta0), (bot_W1, bot_b1, bot_g1, bot_beta1), (bot_W2, bot_b2, bot_g2, bot_beta2)]
        top = [(top_W0, top_b0, top_g0, top_beta0), (top_W1, top_b1, top_g1, top_beta1), (top_W2, top_b2, top_g2, top_beta2)]
        return _forward(sparse_inputs, dense_inputs, emb_tables, bot, top)
    y = _L0_rec_ref(r_sparse_inputs, r_dense_inputs, L0_rec_emb_tables, L0_rec_bot_W0, L0_rec_bot_b0, L0_rec_bot_g0, L0_rec_bot_beta0, L0_rec_bot_W1, L0_rec_bot_b1, L0_rec_bot_g1, L0_rec_bot_beta1, L0_rec_bot_W2, L0_rec_bot_b2, L0_rec_bot_g2, L0_rec_bot_beta2, L0_rec_top_W0, L0_rec_top_b0, L0_rec_top_g0, L0_rec_top_beta0, L0_rec_top_W1, L0_rec_top_b1, L0_rec_top_g1, L0_rec_top_beta1, L0_rec_top_W2, L0_rec_top_b2, L0_rec_top_g2, L0_rec_top_beta2)
    return y

_drawn_inputs = setup_inputs


def setup_inputs(seed=0):
    import zlib

    import numpy as np

    out = dict(_drawn_inputs(seed))
    spreads = {'L0_rec_bot_b0': (0.0, 0.1),
     'L0_rec_bot_g0': (1.0, 0.2),
     'L0_rec_bot_beta0': (0.0, 0.1),
     'L0_rec_bot_b1': (0.0, 0.1),
     'L0_rec_bot_g1': (1.0, 0.2),
     'L0_rec_bot_beta1': (0.0, 0.1),
     'L0_rec_bot_b2': (0.0, 0.1),
     'L0_rec_bot_g2': (1.0, 0.2),
     'L0_rec_bot_beta2': (0.0, 0.1),
     'L0_rec_top_b0': (0.0, 0.1),
     'L0_rec_top_g0': (1.0, 0.2),
     'L0_rec_top_beta0': (0.0, 0.302),
     'L0_rec_top_b1': (0.0, 0.322),
     'L0_rec_top_g1': (1.0, 0.2),
     'L0_rec_top_beta1': (0.0, 0.8)}
    factors = {}
    for name, (base, spread) in spreads.items():
        noise = np.random.default_rng([zlib.crc32(name.encode()), seed]).standard_normal(out[name].shape)
        drawn = base * np.exp(spread * noise) if base else spread * noise
        out[name] = jnp.asarray(drawn.astype(out[name].dtype))
    for name, factor in factors.items():
        out[name] = (out[name] * factor).astype(out[name].dtype)
    return out
```

```python
from contextlib import ExitStack

import concourse.bass as bass
from concourse import mybir

F32 = mybir.dt.float32
I32 = mybir.dt.int32
U32 = mybir.dt.uint32
ALU = mybir.AluOpType
ACT = mybir.ActivationFunctionType

P = 128
B = 2048
TILES = B // P
PAIRS = TILES // 2
NF = 26
V = NF + 1
D = 64
VOCAB = 12500
DENSE = 13
H0, H1 = 512, 256
K0, K1 = H0 // P, H1 // P
EPS = 1e-5

QUAD = 32
NQ = P // QUAD
ZC = 7
GROUP = 4
GROUPS = -(-NF // GROUP)
ROUNDS = 8
ZM = NF
CHUNK = 512
CHUNKS = B // CHUNK
PW = 2 * NF

PARAMS = {}
for _net in ("bot", "top"):
    for _layer, _w in ((0, K0), (1, K1), (2, 1)):
        for _what in ("b", "g", "beta"):
            PARAMS[_net, _what, _layer] = (sum(w for _, w in PARAMS.values()), _w)
PARAMS["top", "W", 2] = (sum(w for _, w in PARAMS.values()), K1)
NPARAM = sum(w for _, w in PARAMS.values())


def group_tables(g):
    return range(g * GROUP, min((g + 1) * GROUP, NF))


def quadrant_columns(q):
    return min(ZC, NF - ZC * q)


def rec_program(nc, idx, table, dense_t, params, identity, bw0, bw1, bw2, tw0x, twx, tw1, out):
    ctx = ExitStack()
    with ctx:
        def sb(name, shape, dt=F32):
            return ctx.enter_context(nc.sbuf_tensor(name, shape, dt))

        def ps(name, shape):
            return ctx.enter_context(nc.psum_tensor(name, shape, F32))

        def sem(name):
            return ctx.enter_context(nc.semaphore(name))

        idx_raw = sb("idx_raw", [P, TILES * NF], I32)
        idx_neg = sb("idx_neg", [P, TILES * NF])
        idx_wrapped = sb("idx_wrapped", [P, TILES * NF])
        idx_clamped = sb("idx_clamped", [P, TILES * NF])
        table_base = sb("table_base", [P, TILES * NF], I32)
        idx_row = sb("idx_row", [P, (PAIRS + 2) * PW], U32)
        stage = sb("stage", [P, 2, PW], U32)
        emb = sb("emb", [P, 2, NF, 2, D])
        TT = sb("TT", [P, 2, P, QUAD])
        Zs = sb("Zs", [P, ZC, 2 * P])
        xT = sb("xT", [P, PAIRS, P])
        x_raw = sb("x_raw", [P, B])
        hidden0 = sb("hidden0", [P, K0, B])
        hidden1 = sb("hidden1", [P, K1, B])
        dense_sb = sb("dense_sb", [DENSE, B])
        par = sb("par", [P, NPARAM])
        ident = sb("ident", [P, P])
        bw0_sb = sb("bw0_sb", [DENSE, H0])
        w1_sb = {"bot": sb("bw1_sb", [P, K0, H1]), "top": sb("tw1_sb", [P, K0, H1])}
        w1_scaled = sb("w1_scaled", [P, K0, H1])
        bw2_sb = sb("bw2_sb", [P, K1, 2 * D])
        w2_scaled = sb("w2_scaled", [P, K1, 2 * D])
        tw0_sb = sb("tw0_sb", [P, ZC, H0])
        twx_sb = sb("twx_sb", [P, 2, H0])
        stats = {("bot", 0): sb("stats_b0", [P, K0, CHUNKS, 6]), ("bot", 1): sb("stats_b1", [P, K1, CHUNKS, 6]),
                 ("bot", 2): sb("stats_b2", [P, 1, CHUNKS, 6]), ("top", 0): sb("stats_t0", [P, K0, PAIRS, 6]),
                 ("top", 1): sb("stats_t1", [P, K1, CHUNKS, 6])}
        norm = {key: sb("norm_%s%d" % key, [P, 10, K0]) for key in
                [(n, l) for n in ("bot", "top") for l in range(3)]}
        moments = {key: sb("moments_%s%d" % key, [P, K0, 2]) for key in stats}
        bias1 = {"bot": sb("bias1_bot", [P, K1]), "top": sb("bias1_top", [P, K1])}
        bias2 = {"bot": sb("bias2_bot", [P, 1]), "top": sb("bias2_top", [P, 1])}
        shift_w2 = sb("shift_w2", [P, K1])
        tw2_scaled = sb("tw2_scaled", [P, K1])
        eps_sb = sb("eps_sb", [P, 1])
        ones = sb("ones", [P, P])
        mean_of = sb("mean_of", [P, P])
        logit_raw = sb("logit_raw", [P, TILES])
        logit_sum = sb("logit_sum", [P, 1])
        logit_mid = sb("logit_mid", [P, TILES])
        logit_sq = sb("logit_sq", [P, TILES])
        sq_sum = sb("sq_sum", [P, 1])
        prob = sb("prob", [P, TILES])

        tr_bank = [ps("tr_bank%d" % k, [P, GROUP * P]) for k in range(2)]
        z_bank = [ps("z_bank%d" % k, [P, 2, 512]) for k in range(2)]
        l0_bank = [ps("l0_bank%d" % k, [P, 2, 2 * P]) for k in range(2)]
        out_bank = [z_bank[0][:, 0, :], z_bank[0][:, 1, :], z_bank[1][:, 0, :], z_bank[1][:, 1, :]]
        small = tr_bank[1]

        idx_loaded = sem("idx_loaded")
        bottom_loaded = sem("bottom_loaded")
        bw1_loaded = sem("bw1_loaded")
        ident_loaded = sem("ident_loaded")
        top_loaded = sem("top_loaded")
        base_ready = sem("base_ready")
        idx_step = sem("idx_step")
        cleared = sem("cleared")
        consts_ready = sem("consts_ready")
        slot_open = sem("slot_open")
        pair_started = sem("pair_started")
        landed = [[sem("landed%d_%d" % (s, g)) for g in range(GROUPS)] for s in range(2)]
        transposed = sem("transposed")
        tt_written = sem("tt_written")
        tt_x_written = sem("tt_x_written")
        z_done = sem("z_done")
        z_taken_v = sem("z_taken_v")
        z_taken_a = sem("z_taken_a")
        l0_done = sem("l0_done")
        l0_relu = sem("l0_relu")
        top0_stats = sem("top0_stats")
        mm_done = {k: sem("mm_done_%s%d" % k) for k in (("bot", 0), ("bot", 1), ("bot", 2), ("top", 1))}
        relu_done = {k: sem("relu_done_%s%d" % k) for k in mm_done}
        stats_done = {k: sem("stats_done_%s%d" % k) for k in mm_done}
        bn_step = {k: sem("bn_step_%s%d" % k) for k in norm}
        var_ready = {k: sem("var_ready_%s%d" % k) for k in norm}
        std_ready = {k: sem("std_ready_%s%d" % k) for k in norm}
        coef_ready = {k: sem("coef_ready_%s%d" % k) for k in norm}
        scaled_v = {k: sem("scaled_v_%s%d" % k) for k in (("bot", 0), ("bot", 1), ("top", 0), ("top", 1))}
        scaled_a = {k: sem("scaled_a_%s%d" % k) for k in (("bot", 0), ("top", 0))}
        fold_done = {k: sem("fold_done_%s%d" % k) for k in scaled_v}
        bias_ready = {k: sem("bias_ready_%s%d" % k) for k in scaled_v}
        x_ready = sem("x_ready")
        logits_done = sem("logits_done")
        logit_step = sem("logit_step")
        mean_done = sem("mean_done")
        sqmean_done = sem("sqmean_done")
        prob_ready = sem("prob_ready")
        stored = sem("stored")

        def p_col(net, what, layer):
            at, width = PARAMS[net, what, layer]
            return par[:, at:at + width]

        def layer_width(net, layer):
            return PARAMS[net, "b", layer][1]

        def take_blocks(copy, r, quadrants):
            for j in quadrants:
                src = z_bank[r % 2][QUAD * j:QUAD * j + V, :, 0:4 * NQ * ZM].rearrange(
                    "p h (g c) -> p h g c", g=4)
                for q in range(NQ):
                    w = quadrant_columns(q)
                    dst = Zs[QUAD * q:QUAD * q + V, 0:w, :].rearrange(
                        "p c (h x j) -> p h x j c", h=2, j=NQ)[:, :, 4 * r:4 * r + 4, j, :]
                    last = copy(dst, src[:, :, :, j * ZM + ZC * q:j * ZM + ZC * q + w])
            return last

        def act_copy(dst, src):
            return nc.scalar.activation(dst, src, ACT.Copy)

        block = ctx.enter_context(nc.Block())

        @block.sync
        def _(sp):
            sp.dma_start(idx_raw[:, :], idx).then_inc(idx_loaded, 16)
            sp.dma_start(dense_sb[:, :], dense_t).then_inc(bottom_loaded, 16)
            sp.dma_start(bw0_sb[:, :], bw0).then_inc(bottom_loaded, 16)
            sp.dma_start(par[:, :], params).then_inc(bottom_loaded, 16)
            sp.dma_start(w1_sb["bot"][:, :, :], bw1.rearrange("(k p) n -> p k n", p=P)).then_inc(bw1_loaded, 16)
            for dup in range(2):
                sp.dma_start(bw2_sb[:, :, dup * D:(dup + 1) * D],
                             bw2.rearrange("(k p) n -> p k n", p=P)).then_inc(bw1_loaded, 16)
            sp.dma_start(ident[:, :], identity).then_inc(ident_loaded, 16)
            sp.dma_start(tw0_sb[:, :, :], tw0x).then_inc(top_loaded, 16)
            sp.dma_start(twx_sb[:, :, :], twx).then_inc(top_loaded, 16)
            sp.dma_start(w1_sb["top"][:, :, :], tw1.rearrange("(k p) n -> p k n", p=P)).then_inc(top_loaded, 16)
            sp.wait_ge(prob_ready, 1)
            sp.dma_start(out, prob[:, :]).then_inc(stored, 16)
            sp.wait_ge(stored, 16)

        @block.gpsimd
        def _(pool):
            pool.iota(table_base[:, :], pattern=[[0, TILES], [VOCAB, NF]], base=0,
                      channel_multiplier=0).then_inc(base_ready, 1)
            with pool.Fori(0, PAIRS // 2) as it:
                for s in range(2):
                    pool.wait_ge(slot_open, it * 2 + (s + 1))
                    pool.sem_inc(pair_started, 1)
                    for n in range(NF):
                        for h in range(2):
                            col = h * NF + n
                            pool.indirect_dma_start(
                                out=emb[:, s, n, h, :], out_offset=None, in_=table,
                                in_offset=bass.IndirectOffsetOnAxis(ap=stage[:, s, col:col + 1], axis=0),
                            ).then_inc(landed[s][n // GROUP], 16)

        @block.tensor
        def _(pe):
            def layer_out(net, layer, k):
                if k >= len(out_bank):
                    pe.wait_ge(relu_done[net, layer], k - len(out_bank) + 1)
                return out_bank[k % len(out_bank)]

            def fold_shift(net, weights, layer, width):
                pe.wait_ge(coef_ready[net, layer], 1)
                shift = norm[net, layer][:, 9, :]
                kn = layer_width(net, layer)
                for o in range(width):
                    for k in range(kn):
                        mm = nc.tensor.matmul(small[:, o:o + 1], weights[:, k, o * P:(o + 1) * P],
                                              shift[:, k:k + 1], start=(k == 0), stop=(k == kn - 1))
                mm.then_inc(fold_done[net, layer], 1)

            def layer1(net):
                fold_shift(net, w1_sb[net], 0, K1)
                pe.wait_ge(scaled_v[net, 0], 1)
                pe.wait_ge(scaled_a[net, 0], 1)
                for ch in range(CHUNKS):
                    for o in range(K1):
                        bank = layer_out(net, 1, ch * K1 + o)
                        for k in range(K0):
                            mm = nc.tensor.matmul(bank, w1_scaled[:, k, o * P:(o + 1) * P],
                                                  hidden0[:, k, ch * CHUNK:(ch + 1) * CHUNK],
                                                  start=(k == 0), stop=(k == K0 - 1))
                        mm.then_inc(mm_done[net, 1], 1)

            pe.wait_ge(bottom_loaded, 48)
            for ch in range(CHUNKS):
                for o in range(K0):
                    bank = layer_out("bot", 0, ch * K0 + o)
                    nc.tensor.matmul(bank, bw0_sb[:, o * P:(o + 1) * P], dense_sb[:, ch * CHUNK:(ch + 1) * CHUNK],
                                     start=True, stop=True).then_inc(mm_done["bot", 0], 1)
            pe.wait_ge(bw1_loaded, 48)
            pe.wait_ge(relu_done["bot", 0], CHUNKS * K0)
            layer1("bot")
            pe.wait_ge(bias_ready["bot", 0], 1)
            fold_shift("bot", bw2_sb, 1, 1)
            pe.wait_ge(scaled_v["bot", 1], 1)
            pe.wait_ge(relu_done["bot", 1], CHUNKS * K1)
            for ch in range(CHUNKS):
                bank = layer_out("bot", 2, ch)
                for k in range(K1):
                    mm = nc.tensor.matmul(bank, w2_scaled[:, k, :], hidden1[:, k, ch * CHUNK:(ch + 1) * CHUNK],
                                          start=(k == 0), stop=(k == K1 - 1))
                mm.then_inc(mm_done["bot", 2], 1)

            pe.wait_ge(bias_ready["bot", 1], 1)
            pe.wait_ge(ident_loaded, 16)
            pe.wait_ge(top_loaded, 48)
            pe.wait_ge(cleared, 2)
            with pe.Fori(0, PAIRS // 2) as it:
                for s in range(2):
                    i = it * 2 + s
                    for g in range(GROUPS):
                        tables = group_tables(g)
                        pe.wait_ge(landed[s][g], (it + 1) * (len(tables) * 2 * 16))
                        if g >= 2:
                            pe.wait_ge(tt_written, i * GROUPS + (g - 1))
                        bank = tr_bank[(s * GROUPS + g) % 2]
                        for k, n in enumerate(tables):
                            tr = nc.tensor.transpose(bank[:, k * P:(k + 1) * P],
                                                     emb[:, s, n, :, :].rearrange("p h d -> p (h d)"), ident[:, :])
                        tr.then_inc(transposed, 1)
                    pe.wait_ge(tt_written, (i + 1) * GROUPS)
                    pe.wait_ge(tt_x_written, i + 1)
                    for r in range(ROUNDS):
                        if r >= 2:
                            pe.wait_ge(z_taken_v, i * ROUNDS + (r - 1))
                            pe.wait_ge(z_taken_a, i * ROUNDS + (r - 1))
                        for g in range(4):
                            for h in range(2):
                                b = (4 * r + g) * NQ
                                four = TT[h * D:(h + 1) * D, s, b:b + NQ, :]
                                mm = nc.tensor.matmul(z_bank[r % 2][:, h, g * NQ * ZM:(g + 1) * NQ * ZM],
                                                      four.rearrange("p j v -> p (j v)"), four[:, :, 1:V],
                                                      start=True, stop=True)
                        mm.then_inc(z_done, 1)
                    pe.wait_ge(z_taken_v, (i + 1) * ROUNDS)
                    pe.wait_ge(z_taken_a, (i + 1) * ROUNDS)
                    for o in range(K0):
                        acc = l0_bank[o // 2][:, o % 2, :]
                        cols = slice(o * P, (o + 1) * P)
                        for c in range(ZC):
                            nc.tensor.matmul(acc, tw0_sb[:, c, cols], Zs[:, c, :], start=(c == 0), stop=False)
                        for h in range(2):
                            mm = nc.tensor.matmul(acc[:, h * P:(h + 1) * P], twx_sb[:, h, cols],
                                                  xT[:, bass.ds(i, 1), :].rearrange("p a b -> p (a b)"),
                                                  start=False, stop=(h == 1))
                        if o % 2:
                            mm.then_inc(l0_done, 1)
                    pe.wait_ge(l0_relu, (i + 1) * K0)

            layer1("top")
            pe.wait_ge(coef_ready["top", 1], 1)
            pe.wait_ge(scaled_v["top", 1], 2)
            pe.wait_ge(bias_ready["top", 0], 1)
            for k in range(K1):
                mm = nc.tensor.matmul(small[:, 8:9], ones[:, :], shift_w2[:, k:k + 1],
                                      start=(k == 0), stop=(k == K1 - 1))
            mm.then_inc(fold_done["top", 1], 1)
            pe.wait_ge(relu_done["top", 1], CHUNKS * K1)
            for t in range(TILES):
                for k in range(K1):
                    mm = nc.tensor.matmul(out_bank[0][:, t:t + 1], hidden1[:, k, t * P:(t + 1) * P],
                                          tw2_scaled[:, k:k + 1], start=(k == 0), stop=(k == K1 - 1))
            mm.then_inc(logits_done, 1)
            pe.wait_ge(logit_step, 2)
            nc.tensor.matmul(out_bank[1][:, 0:1], mean_of[:, :], logit_sum[:, :],
                             start=True, stop=True).then_inc(mean_done, 1)
            pe.wait_ge(logit_step, 4)
            nc.tensor.matmul(out_bank[2][:, 0:1], mean_of[:, :], sq_sum[:, :],
                             start=True, stop=True).then_inc(sqmean_done, 1)

        @block.scalar
        def _(act):
            def relu_blocks(net, layer, blocks, dest, bias):
                for n, (o, ch) in enumerate(blocks):
                    act.wait_ge(mm_done[net, layer], n + 1)
                    nc.scalar.activation(dest[:, o, ch * CHUNK:(ch + 1) * CHUNK], out_bank[n % len(out_bank)],
                                         ACT.Relu, bias=bias[:, o:o + 1]).then_inc(relu_done[net, layer], 1)

            def std(net, layer):
                act.wait_ge(var_ready[net, layer], 1)
                w = layer_width(net, layer)
                nc.scalar.activation(norm[net, layer][:, 1, 0:w], norm[net, layer][:, 0, 0:w],
                                     ACT.Sqrt).then_inc(std_ready[net, layer], 1)

            def layer1(net):
                std(net, 0)
                act.wait_ge(coef_ready[net, 0], 1)
                for k in range(K0 // 2, K0):
                    last = nc.scalar.activation(w1_scaled[:, k, :], w1_sb[net][:, k, :], ACT.Copy,
                                                scale=norm[net, 0][:, 8, k:k + 1])
                last.then_inc(scaled_a[net, 0], 1)
                act.wait_ge(bias_ready[net, 0], 1)
                relu_blocks(net, 1, [(o, ch) for ch in range(CHUNKS) for o in range(K1)], hidden1, bias1[net])

            act.wait_ge(bottom_loaded, 48)
            relu_blocks("bot", 0, [(o, ch) for ch in range(CHUNKS) for o in range(K0)], hidden0,
                        p_col("bot", "b", 0))
            act.wait_ge(bw1_loaded, 48)
            layer1("bot")
            std("bot", 1)
            act.wait_ge(bias_ready["bot", 1], 1)
            relu_blocks("bot", 2, [(0, ch) for ch in range(CHUNKS)], x_raw[:, :].rearrange("p (a b) -> p a b", a=1),
                        bias2["bot"])
            std("bot", 2)
            act.wait_ge(coef_ready["bot", 2], 1)
            for h in range(2):
                rows = slice(h * D, (h + 1) * D)
                nc.scalar.activation(xT[rows, :, :],
                                     x_raw[rows, :].rearrange("p (i h b) -> p i h b", h=2, b=P)[:, :, h, :],
                                     ACT.Identity, scale=norm["bot", 2][rows, 8, 0:1],
                                     bias=norm["bot", 2][rows, 9, 0:1]).then_inc(x_ready, 1)

            act.wait_ge(x_ready, 2)
            act.wait_ge(cleared, 2)
            with act.Fori(0, PAIRS // 2) as it:
                for s in range(2):
                    i = it * 2 + s
                    nc.scalar.activation(TT[:, s, :, NF:V].rearrange("p b v -> p (b v)"),
                                         xT[:, bass.ds(i, 1), :].rearrange("p a b -> p (a b)"),
                                         ACT.Copy).then_inc(tt_x_written, 1)
                    for r in range(ROUNDS):
                        act.wait_ge(z_done, i * ROUNDS + (r + 1))
                        last = take_blocks(act_copy, r, (2, 3))
                        last.then_inc(z_taken_a, 1)
                    for o in range(K0):
                        if o % 2 == 0:
                            act.wait_ge(l0_done, i * 2 + (o // 2 + 1))
                        nc.scalar.activation(hidden0[:, o, bass.ds(i * (2 * P), 2 * P)], l0_bank[o // 2][:, o % 2, :],
                                             ACT.Relu, bias=p_col("top", "b", 0)[:, o:o + 1]).then_inc(l0_relu, 1)

            act.wait_ge(top_loaded, 48)
            layer1("top")
            std("top", 1)
            std("top", 2)
            act.wait_ge(coef_ready["top", 2], 1)
            nc.scalar.activation(prob[:, :], logit_mid[:, :], ACT.Sigmoid, scale=norm["top", 2][:, 8, 0:1],
                                 bias=p_col("top", "beta", 2)).then_inc(prob_ready, 1)

        @block.vector
        def _(dve):
            def chain(semaphore, count):
                done = [count]

                def step(ins):
                    done[0] += 1
                    ins.then_inc(semaphore, 1)
                    dve.wait_ge(semaphore, done[0])
                return step

            def block_stats(net, layer, blocks, src):
                for n, (o, ch) in enumerate(blocks):
                    dve.wait_ge(relu_done[net, layer], n + 1)
                    last = nc.vector.bn_stats(stats[net, layer][:, o, ch, :],
                                              src[:, o, ch * CHUNK:(ch + 1) * CHUNK])
                last.then_inc(stats_done[net, layer], 1)
                dve.wait_ge(stats_done[net, layer], 1)

            def rstd(net, layer, step):
                v = norm[net, layer]
                w = layer_width(net, layer)
                dve.wait_ge(std_ready[net, layer], 1)
                step(nc.vector.reciprocal(v[:, 2, 0:w], v[:, 1, 0:w]))
                step(nc.vector.tensor_tensor(v[:, 3, 0:w], v[:, 2, 0:w], v[:, 2, 0:w], ALU.mult))
                step(nc.vector.tensor_tensor(v[:, 4, 0:w], v[:, 3, 0:w], v[:, 0, 0:w], ALU.mult))
                step(nc.vector.tensor_scalar(v[:, 5, 0:w], v[:, 4, 0:w], -0.5, 1.5, ALU.mult, ALU.add))
                step(nc.vector.tensor_tensor(v[:, 6, 0:w], v[:, 5, 0:w], v[:, 2, 0:w], ALU.mult))

            def coefficients(net, layer):
                v = norm[net, layer]
                w = layer_width(net, layer)
                step = chain(bn_step[net, layer], 0)
                for k in range(w):
                    last = nc.vector.bn_aggr(moments[net, layer][:, k, :],
                                             stats[net, layer][:, k, :, :].rearrange("p a b -> p (a b)"))
                step(last)
                mean, var = moments[net, layer][:, 0:w, 0], moments[net, layer][:, 0:w, 1]
                nc.vector.tensor_scalar_add(v[:, 0, 0:w], var, EPS).then_inc(var_ready[net, layer], 1)
                rstd(net, layer, step)
                step(nc.vector.tensor_tensor(v[:, 8, 0:w], v[:, 6, 0:w], p_col(net, "g", layer), ALU.mult))
                step(nc.vector.tensor_tensor(v[:, 7, 0:w], v[:, 8, 0:w], mean, ALU.mult))
                nc.vector.tensor_tensor(v[:, 9, 0:w], p_col(net, "beta", layer), v[:, 7, 0:w],
                                        ALU.subtract).then_inc(coef_ready[net, layer], 1)

            def layer1(net):
                coefficients(net, 0)
                for k in range(K0 // 2):
                    last = nc.vector.tensor_scalar_mul(w1_scaled[:, k, :], w1_sb[net][:, k, :],
                                                       norm[net, 0][:, 8, k:k + 1])
                last.then_inc(scaled_v[net, 0], 1)
                dve.wait_ge(fold_done[net, 0], 1)
                nc.vector.tensor_tensor(bias1[net][:, :], small[:, 0:K1], p_col(net, "b", 1),
                                        ALU.add).then_inc(bias_ready[net, 0], 1)
                block_stats(net, 1, [(o, ch) for ch in range(CHUNKS) for o in range(K1)], hidden1)

            dve.wait_ge(idx_loaded, 16)
            step = chain(idx_step, 0)
            step(nc.vector.tensor_scalar(idx_neg[:, :], idx_raw[:, :], 0.0, float(VOCAB), ALU.is_lt, ALU.mult))
            step(nc.vector.tensor_tensor(idx_wrapped[:, :], idx_raw[:, :], idx_neg[:, :], ALU.add))
            step(nc.vector.tensor_scalar(idx_clamped[:, :], idx_wrapped[:, :], 0.0, float(VOCAB - 1),
                                         ALU.max, ALU.min))
            dve.wait_ge(base_ready, 1)
            step(nc.vector.tensor_tensor(idx_row[:, 0:PAIRS * PW], idx_clamped[:, :], table_base[:, :], ALU.add))
            for s in range(2):
                nc.vector.tensor_copy(stage[:, s, :], idx_row[:, s * PW:(s + 1) * PW]).then_inc(slot_open, 1)
            nc.vector.memset(TT[:, :, :, V:QUAD].rearrange("p s b v -> p (s b) v"), 0.0).then_inc(cleared, 1)
            nc.vector.memset(Zs[:, :, :], 0.0).then_inc(cleared, 1)
            nc.vector.memset(idx_row[:, PAIRS * PW:(PAIRS + 2) * PW], 0).then_inc(consts_ready, 1)
            nc.vector.memset(ones[:, :], 1.0).then_inc(consts_ready, 1)
            nc.vector.memset(mean_of[:, :], 1.0 / B).then_inc(consts_ready, 1)
            dve.wait_ge(consts_ready, 3)

            dve.wait_ge(bottom_loaded, 48)
            block_stats("bot", 0, [(o, ch) for ch in range(CHUNKS) for o in range(K0)], hidden0)
            dve.wait_ge(bw1_loaded, 48)
            layer1("bot")
            coefficients("bot", 1)
            for k in range(K1):
                last = nc.vector.tensor_scalar_mul(w2_scaled[:, k, :], bw2_sb[:, k, :], norm["bot", 1][:, 8, k:k + 1])
            last.then_inc(scaled_v["bot", 1], 1)
            dve.wait_ge(fold_done["bot", 1], 1)
            nc.vector.tensor_tensor(bias2["bot"][:, :], small[:, 0:1], p_col("bot", "b", 2),
                                    ALU.add).then_inc(bias_ready["bot", 1], 1)
            block_stats("bot", 2, [(0, ch) for ch in range(CHUNKS)], x_raw[:, :].rearrange("p (a b) -> p a b", a=1))
            coefficients("bot", 2)

            dve.wait_ge(cleared, 2)
            with dve.Fori(0, PAIRS // 2) as it:
                for s in range(2):
                    i = it * 2 + s
                    for g in range(GROUPS):
                        tables = group_tables(g)
                        n0, w = tables[0], len(tables)
                        dve.wait_ge(transposed, i * GROUPS + (g + 1))
                        nc.vector.tensor_copy(TT[:, s, :, n0:n0 + w].rearrange("p b n -> p n b"),
                                              tr_bank[(s * GROUPS + g) % 2][:, 0:w * P].rearrange(
                                                  "p (n b) -> p n b", n=w)).then_inc(tt_written, 1)
                    nc.vector.tensor_copy(stage[:, s, :], idx_row[:, bass.ds((i + 2) * PW, PW)]).then_inc(slot_open, 1)
                    for r in range(ROUNDS):
                        dve.wait_ge(z_done, i * ROUNDS + (r + 1))
                        last = take_blocks(nc.vector.tensor_copy, r, (0, 1))
                        last.then_inc(z_taken_v, 1)
                    for o in range(K0):
                        dve.wait_ge(l0_relu, i * K0 + (o + 1))
                        nc.vector.bn_stats(stats["top", 0][:, o, bass.ds(i, 1), :].rearrange("p a b -> p (a b)"),
                                           hidden0[:, o, bass.ds(i * (2 * P), 2 * P)]).then_inc(top0_stats, 1)

            dve.wait_ge(top0_stats, PAIRS * K0)
            layer1("top")
            coefficients("top", 1)
            shift = norm["top", 1][:, 9, 0:K1]
            dve.wait_ge(coef_ready["top", 1], 1)
            nc.vector.tensor_tensor(shift_w2[:, :], shift, p_col("top", "W", 2), ALU.mult).then_inc(scaled_v["top", 1], 1)
            nc.vector.tensor_tensor(tw2_scaled[:, :], norm["top", 1][:, 8, 0:K1], p_col("top", "W", 2),
                                    ALU.mult).then_inc(scaled_v["top", 1], 1)
            dve.wait_ge(fold_done["top", 1], 1)
            nc.vector.tensor_tensor(bias2["top"][:, :], small[:, 8:9], p_col("top", "b", 2),
                                    ALU.add).then_inc(bias_ready["top", 1], 1)
            dve.wait_ge(bias_ready["top", 1], 1)
            step = chain(logit_step, 0)
            dve.wait_ge(logits_done, 1)
            step(nc.vector.tensor_scalar(logit_raw[:, :], out_bank[0][:, 0:TILES], bias2["top"][:, 0:1], 0.0,
                                         ALU.add, ALU.max))
            step(nc.vector.reduce_sum(logit_sum[:, :], logit_raw[:, :], mybir.AxisListType.X))
            dve.wait_ge(mean_done, 1)
            step(nc.vector.tensor_scalar(logit_mid[:, :], logit_raw[:, :], out_bank[1][:, 0:1], None, ALU.subtract))
            step(nc.vector.tensor_tensor_reduce(out=logit_sq[:, :], in0=logit_mid[:, :], in1=logit_mid[:, :],
                                                scale=1.0, scalar=0.0, op0=ALU.mult, op1=ALU.add,
                                                accum_out=sq_sum[:, :]))
            dve.wait_ge(sqmean_done, 1)
            v = norm["top", 2]
            nc.vector.tensor_scalar_add(v[:, 0, 0:1], out_bank[2][:, 0:1], EPS).then_inc(var_ready["top", 2], 1)
            rstd("top", 2, chain(bn_step["top", 2], 0))
            nc.vector.tensor_tensor(v[:, 8, 0:1], v[:, 6, 0:1], p_col("top", "g", 2),
                                    ALU.mult).then_inc(coef_ready["top", 2], 1)


def kernel(**inputs):
    import numpy as np
    import concourse.bacc as bacc
    from concourse import mybir as mb
    from concourse.bass_utils import run_bass_kernel_spmd as run

    def get(name):
        return np.ascontiguousarray(inputs[name])

    def columns(vec):
        return vec.reshape(-1, P).T

    dense_t = get("r_dense_inputs").reshape(P, TILES, DENSE).transpose(2, 1, 0).reshape(DENSE, B)
    params = np.zeros((P, NPARAM), np.float32)
    for (net, what, layer), (at, width) in PARAMS.items():
        vec = get("L0_rec_%s_%s%d" % (net, what, layer)).reshape(-1)
        if vec.size < P:
            vec = np.tile(vec, P // vec.size)
        params[:, at:at + width] = columns(vec)
    w0 = get("L0_rec_top_W0")
    twx = np.zeros((P, 2, H0), np.float32)
    tw0x = np.zeros((P, ZC, H0), np.float32)
    for h in range(2):
        twx[h * D:(h + 1) * D, h] = w0[0:D]
    for row, (n, m) in enumerate(zip(*np.triu_indices(V, k=1))):
        q, c = divmod(m - 1, ZC)
        tw0x[QUAD * q + n, c] = w0[D + row]

    arrays = {
        "idx": get("r_sparse_inputs").reshape(P, TILES * NF),
        "table": get("L0_rec_emb_tables").reshape(NF * VOCAB, D),
        "dense_t": np.ascontiguousarray(dense_t),
        "params": params,
        "identity": np.eye(P, dtype=np.float32),
        "bw0": get("L0_rec_bot_W0"), "bw1": get("L0_rec_bot_W1"), "bw2": get("L0_rec_bot_W2"),
        "tw0x": tw0x, "twx": twx, "tw1": get("L0_rec_top_W1"),
    }
    nc = bacc.Bacc("TRN2", target_bir_lowering=False, num_devices=1)
    args = [nc.dram_tensor(k, a.shape, mb.dt.from_np(a.dtype), kind="ExternalInput").ap() for k, a in arrays.items()]
    out = nc.dram_tensor("out", (P, TILES), mb.dt.float32, kind="ExternalOutput").ap()
    rec_program(nc, *args, out)
    result = run(nc, [arrays], core_ids=[0])
    return result.results[0]["out"].reshape(B, 1)
```

```python
from contextlib import ExitStack

import concourse.bass as bass
from concourse import mybir

F32 = mybir.dt.float32
I32 = mybir.dt.int32
U32 = mybir.dt.uint32
ALU = mybir.AluOpType
ACT = mybir.ActivationFunctionType

P = 128
B = 2048
TILES = B // P
PAIRS = TILES // 2
NF = 26
V = NF + 1
D = 64
VOCAB = 12500
DENSE = 13
H0, H1 = 512, 256
K0, K1 = H0 // P, H1 // P
EPS = 1e-5

QUAD = 32
NQ = P // QUAD
ZC = 7
PART = P // 2
PARTS = P // PART
TP = NF // 2
GROUP = 4
GROUPS = -(-TP // GROUP)
ROUNDS = 2 * PARTS
RX = PART // NQ
ZM = NF
CHUNK = 512
CHUNKS = B // CHUNK
CT = CHUNK // P
PW = 2 * NF

PARAMS = {}
for _net in ("bot", "top"):
    for _layer, _w in ((0, K0), (1, K1), (2, 1)):
        for _what in ("b", "g", "beta"):
            PARAMS[_net, _what, _layer] = (sum(w for _, w in PARAMS.values()), _w)
PARAMS["top", "W", 2] = (sum(w for _, w in PARAMS.values()), K1)
NPARAM = sum(w for _, w in PARAMS.values())


def group_pairs(g):
    return range(g * GROUP, min((g + 1) * GROUP, TP))


def quadrant_columns(q):
    return min(ZC, NF - ZC * q)


def rec_program(nc, idx, table, dense_t, params, identity, bw0, bw1, bw2, tw0x, twx, tw1, out):
    ctx = ExitStack()
    with ctx:
        def sb(name, shape, dt=F32):
            return ctx.enter_context(nc.sbuf_tensor(name, shape, dt))

        def ps(name, shape):
            return ctx.enter_context(nc.psum_tensor(name, shape, F32))

        def sem(name):
            return ctx.enter_context(nc.semaphore(name))

        idx_raw = sb("idx_raw", [P, TILES * NF], I32)
        idx_neg = sb("idx_neg", [P, TILES * NF])
        idx_wrapped = sb("idx_wrapped", [P, TILES * NF])
        idx_clamped = sb("idx_clamped", [P, TILES * NF])
        table_base = sb("table_base", [P, TILES * NF], I32)
        idx_row = sb("idx_row", [P, (PAIRS + 2) * PW], U32)
        stage = sb("stage", [P, 2, PW], U32)
        emb = sb("emb", [P, 2, PARTS, TP, 2, D])
        TT = sb("TT", [P, 2, P, V])
        Zs = sb("Zs", [P, ZC, 2 * P])
        x_all = sb("x_all", [P, B])
        x_raw = sb("x_raw", [P, B])
        hidden0 = sb("hidden0", [P, K0, B])
        hidden1 = sb("hidden1", [P, K1, B])
        dense_sb = sb("dense_sb", [DENSE, B])
        par = sb("par", [P, NPARAM])
        ident = sb("ident", [P, P])
        bw0_sb = sb("bw0_sb", [DENSE, H0])
        w1_sb = {"bot": sb("bw1_sb", [P, K0, H1]), "top": sb("tw1_sb", [P, K0, H1])}
        w1_scaled = sb("w1_scaled", [P, K0, H1])
        bw2_sb = sb("bw2_sb", [P, K1, 2 * D])
        w2_scaled = sb("w2_scaled", [P, K1, 2 * D])
        tw0_sb = sb("tw0_sb", [P, ZC, H0])
        twx_sb = sb("twx_sb", [P, H0])
        stats = {("bot", 0): sb("stats_b0", [P, K0, CHUNKS, 6]), ("bot", 1): sb("stats_b1", [P, K1, CHUNKS, 6]),
                 ("bot", 2): sb("stats_b2", [P, 1, CHUNKS, 6]), ("top", 0): sb("stats_t0", [P, K0, PAIRS, 6]),
                 ("top", 1): sb("stats_t1", [P, K1, CHUNKS, 6])}
        norm = {key: sb("norm_%s%d" % key, [P, 10, K0]) for key in
                [(n, l) for n in ("bot", "top") for l in range(3)]}
        moments = {key: sb("moments_%s%d" % key, [P, K0, 2]) for key in stats}
        bias1 = {"bot": sb("bias1_bot", [P, K1]), "top": sb("bias1_top", [P, K1])}
        bias2 = {"bot": sb("bias2_bot", [P, 1]), "top": sb("bias2_top", [P, 1])}
        shift_w2 = sb("shift_w2", [P, K1])
        tw2_rep = sb("tw2_rep", [P, K1, QUAD])
        ones = sb("ones", [P, P])
        mean_of = sb("mean_of", [P, P])
        logits = sb("logits", [P, CHUNK])
        logit_sum = sb("logit_sum", [P, 1])
        neg_mean = sb("neg_mean", [P, 1])
        logit_sq = sb("logit_sq", [P, CHUNK])
        sq_sum = sb("sq_sum", [P, 1])
        prob = sb("prob", [P, P, CT])

        tr_bank = [ps("tr_bank%d" % k, [P, GROUP * P]) for k in range(2)]
        z_bank = [ps("z_bank%d" % k, [P, 512]) for k in range(ROUNDS)]
        l0_bank = [ps("l0_bank%d" % k, [P, 512]) for k in range(2)]
        acc_bank = l0_bank + tr_bank
        out_bank = [bank[:, :] for bank in z_bank]
        small = tr_bank[1]

        idx_loaded = sem("idx_loaded")
        bottom_loaded = sem("bottom_loaded")
        bw1_loaded = sem("bw1_loaded")
        ident_loaded = sem("ident_loaded")
        top_loaded = sem("top_loaded")
        base_ready = sem("base_ready")
        idx_step = sem("idx_step")
        cleared = sem("cleared")
        consts_ready = sem("consts_ready")
        slot_open = sem("slot_open")
        pair_started = sem("pair_started")
        landed = [[[sem("landed%d_%d_%d" % (s, a, g)) for g in range(GROUPS)] for a in range(PARTS)]
                  for s in range(2)]
        transposed = sem("transposed")
        tt_written = sem("tt_written")
        tt_x_written = sem("tt_x_written")
        z_started = sem("z_started")
        z_done = sem("z_done")
        z_taken_v = sem("z_taken_v")
        z_taken_a = sem("z_taken_a")
        l0_done = sem("l0_done")
        l0_relu = sem("l0_relu")
        top0_stats = sem("top0_stats")
        mm_done = {k: sem("mm_done_%s%d" % k) for k in (("bot", 0), ("bot", 1), ("bot", 2), ("top", 1))}
        relu_done = {k: sem("relu_done_%s%d" % k) for k in mm_done}
        stats_done = {k: sem("stats_done_%s%d" % k) for k in mm_done}
        bn_step = {k: sem("bn_step_%s%d" % k) for k in norm}
        var_ready = {k: sem("var_ready_%s%d" % k) for k in norm}
        std_ready = {k: sem("std_ready_%s%d" % k) for k in norm}
        coef_ready = {k: sem("coef_ready_%s%d" % k) for k in norm}
        scaled_v = {k: sem("scaled_v_%s%d" % k) for k in (("bot", 0), ("bot", 1), ("top", 0), ("top", 1))}
        scaled_a = {k: sem("scaled_a_%s%d" % k) for k in (("bot", 0), ("top", 0))}
        fold_done = {k: sem("fold_done_%s%d" % k) for k in scaled_v}
        bias_ready = {k: sem("bias_ready_%s%d" % k) for k in scaled_v}
        x_ready = sem("x_ready")
        logits_done = sem("logits_done")
        logit_summed = sem("logit_summed")
        mean_ready = sem("mean_ready")
        sq_summed = sem("sq_summed")
        mean_done = sem("mean_done")
        sqmean_done = sem("sqmean_done")
        prob_ready = sem("prob_ready")
        stored = sem("stored")

        def p_col(net, what, layer):
            at, width = PARAMS[net, what, layer]
            return par[:, at:at + width]

        def layer_width(net, layer):
            return PARAMS[net, "b", layer][1]

        def take_blocks(copy, r, quadrants):
            for j in quadrants:
                src = z_bank[r][QUAD * j:QUAD * j + V, 0:RX * ZM].rearrange("p (x c) -> p x c", c=ZM)
                for q in range(NQ):
                    w = quadrant_columns(q)
                    dst = Zs[QUAD * q:QUAD * q + V, 0:w, :].rearrange(
                        "p c (h a x j) -> p h a x j c", h=2, a=PARTS, j=NQ)[:, r % 2, r // 2, :, j, :]
                    last = copy(dst, src[:, :, ZC * q:ZC * q + w])
            return last

        def act_copy(dst, src):
            return nc.scalar.activation(dst, src, ACT.Copy)

        block = ctx.enter_context(nc.Block())

        @block.sync
        def _(sp):
            sp.dma_start(idx_raw[:, :], idx).then_inc(idx_loaded, 16)
            sp.dma_start(dense_sb[:, :], dense_t).then_inc(bottom_loaded, 16)
            sp.dma_start(bw0_sb[:, :], bw0).then_inc(bottom_loaded, 16)
            sp.dma_start(par[:, :], params).then_inc(bottom_loaded, 16)
            sp.dma_start(w1_sb["bot"][:, :, :], bw1.rearrange("(k p) n -> p k n", p=P)).then_inc(bw1_loaded, 16)
            for dup in range(2):
                sp.dma_start(bw2_sb[:, :, dup * D:(dup + 1) * D],
                             bw2.rearrange("(k p) n -> p k n", p=P)).then_inc(bw1_loaded, 16)
            sp.dma_start(ident[:, :], identity).then_inc(ident_loaded, 16)
            sp.dma_start(tw0_sb[:, :, :], tw0x).then_inc(top_loaded, 16)
            sp.dma_start(twx_sb[:, :], twx).then_inc(top_loaded, 16)
            sp.dma_start(w1_sb["top"][:, :, :], tw1.rearrange("(k p) n -> p k n", p=P)).then_inc(top_loaded, 16)
            sp.wait_ge(prob_ready, 1)
            sp.dma_start(out, prob[0:P:QUAD, :, :].rearrange("p a b -> p (a b)")).then_inc(stored, 16)
            sp.wait_ge(stored, 16)

        @block.gpsimd
        def _(pool):
            for e in range(2):
                pool.iota(table_base[e * PART:(e + 1) * PART, :], pattern=[[0, PAIRS * PARTS], [2 * VOCAB, TP], [0, 2]],
                          base=e * VOCAB, channel_multiplier=0).then_inc(base_ready, 1)
            with pool.Fori(0, PAIRS // 2) as it:
                for s in range(2):
                    pool.wait_ge(slot_open, it * 2 + (s + 1))
                    pool.sem_inc(pair_started, 1)
                    for a in range(PARTS):
                        for k in range(TP):
                            for h in range(2):
                                col = (a * TP + k) * 2 + h
                                pool.indirect_dma_start(
                                    out=emb[:, s, a, k, h, :], out_offset=None, in_=table,
                                    in_offset=bass.IndirectOffsetOnAxis(ap=stage[:, s, col:col + 1], axis=0),
                                ).then_inc(landed[s][a][k // GROUP], 16)

        @block.tensor
        def _(pe):
            def layer_out(net, layer, k):
                if k >= len(out_bank):
                    pe.wait_ge(relu_done[net, layer], k - len(out_bank) + 1)
                return out_bank[k % len(out_bank)]

            def fold_shift(net, weights, layer, width):
                pe.wait_ge(coef_ready[net, layer], 1)
                shift = norm[net, layer][:, 9, :]
                kn = layer_width(net, layer)
                for o in range(width):
                    for k in range(kn):
                        mm = nc.tensor.matmul(small[:, o:o + 1], weights[:, k, o * P:(o + 1) * P],
                                              shift[:, k:k + 1], start=(k == 0), stop=(k == kn - 1))
                mm.then_inc(fold_done[net, layer], 1)

            def layer1(net):
                fold_shift(net, w1_sb[net], 0, K1)
                pe.wait_ge(scaled_v[net, 0], 1)
                pe.wait_ge(scaled_a[net, 0], 1)
                for ch in range(CHUNKS):
                    for o in range(K1):
                        bank = layer_out(net, 1, ch * K1 + o)
                        for k in range(K0):
                            mm = nc.tensor.matmul(bank, w1_scaled[:, k, o * P:(o + 1) * P],
                                                  hidden0[:, k, ch * CHUNK:(ch + 1) * CHUNK],
                                                  start=(k == 0), stop=(k == K0 - 1))
                        mm.then_inc(mm_done[net, 1], 1)

            pe.wait_ge(bottom_loaded, 48)
            for ch in range(CHUNKS):
                for o in range(K0):
                    bank = layer_out("bot", 0, ch * K0 + o)
                    nc.tensor.matmul(bank, bw0_sb[:, o * P:(o + 1) * P], dense_sb[:, ch * CHUNK:(ch + 1) * CHUNK],
                                     start=True, stop=True).then_inc(mm_done["bot", 0], 1)
            pe.wait_ge(bw1_loaded, 48)
            pe.wait_ge(relu_done["bot", 0], CHUNKS * K0)
            layer1("bot")
            pe.wait_ge(bias_ready["bot", 0], 1)
            fold_shift("bot", bw2_sb, 1, 1)
            pe.wait_ge(scaled_v["bot", 1], 1)
            pe.wait_ge(relu_done["bot", 1], CHUNKS * K1)
            for ch in range(CHUNKS):
                bank = layer_out("bot", 2, ch)
                for k in range(K1):
                    mm = nc.tensor.matmul(bank, w2_scaled[:, k, :], hidden1[:, k, ch * CHUNK:(ch + 1) * CHUNK],
                                          start=(k == 0), stop=(k == K1 - 1))
                mm.then_inc(mm_done["bot", 2], 1)

            pe.wait_ge(bias_ready["bot", 1], 1)
            pe.wait_ge(ident_loaded, 16)
            pe.wait_ge(top_loaded, 48)
            pe.wait_ge(cleared, 1)
            with pe.Fori(0, PAIRS // 2) as it:
                for s in range(2):
                    i = it * 2 + s
                    for a in range(PARTS):
                        for g in range(GROUPS):
                            pairs = group_pairs(g)
                            pe.wait_ge(landed[s][a][g], (it + 1) * (len(pairs) * 2 * 16))
                            n = a * GROUPS + g
                            if n >= 2:
                                pe.wait_ge(tt_written, i * (PARTS * GROUPS) + (n - 1))
                            for c, k in enumerate(pairs):
                                tr = nc.tensor.transpose(tr_bank[n % 2][:, c * P:(c + 1) * P],
                                                         emb[:, s, a, k, :, :].rearrange("p h d -> p (h d)"),
                                                         ident[:, :])
                            tr.then_inc(transposed, 1)
                        pe.wait_ge(tt_written, i * (PARTS * GROUPS) + (a + 1) * GROUPS)
                        pe.wait_ge(tt_x_written, i + 1)
                        pe.sem_inc(z_started, 1)
                        for h in range(2):
                            bank = z_bank[a * 2 + h]
                            for x in range(RX):
                                for j in range(NQ):
                                    one = TT[h * D:(h + 1) * D, s, a * PART + x * NQ + j, :]
                                    mm = nc.tensor.matmul(bank[QUAD * j:QUAD * j + V, x * ZM:(x + 1) * ZM],
                                                          one, one[:, 1:V], start=True, stop=True)
                            mm.then_inc(z_done, 1)
                    pe.wait_ge(z_taken_v, (i + 1) * ROUNDS)
                    pe.wait_ge(z_taken_a, (i + 1) * ROUNDS)
                    for o in range(K0):
                        acc = acc_bank[o][:, 0:2 * P]
                        cols = slice(o * P, (o + 1) * P)
                        nc.tensor.matmul(acc, twx_sb[:, cols], x_all[:, bass.ds(i * (2 * P), 2 * P)],
                                         start=True, stop=False)
                        for c in range(ZC):
                            mm = nc.tensor.matmul(acc, tw0_sb[:, c, cols], Zs[:, c, :],
                                                  start=False, stop=(c == ZC - 1))
                        mm.then_inc(l0_done, 1)
                    pe.wait_ge(l0_relu, (i + 1) * K0)

            layer1("top")
            pe.wait_ge(scaled_v["top", 1], 1)
            pe.wait_ge(bias_ready["top", 0], 1)
            for k in range(K1):
                mm = nc.tensor.matmul(small[:, 8:9], ones[:, :], shift_w2[:, k:k + 1],
                                      start=(k == 0), stop=(k == K1 - 1))
            mm.then_inc(fold_done["top", 1], 1)
            pe.wait_ge(scaled_v["top", 1], 2)
            pe.wait_ge(relu_done["top", 1], CHUNKS * K1)
            for k in range(K1):
                for j in range(CHUNKS):
                    mm = nc.tensor.matmul(out_bank[0][QUAD * j:QUAD * (j + 1), :], tw2_rep[:, k, :],
                                          hidden1[:, k, j * CHUNK:(j + 1) * CHUNK],
                                          start=(k == 0), stop=(k == K1 - 1))
            mm.then_inc(logits_done, 1)
            pe.wait_ge(logit_summed, 1)
            nc.tensor.matmul(out_bank[1][:, 0:1], mean_of[:, :], logit_sum[:, :],
                             start=True, stop=True).then_inc(mean_done, 1)
            pe.wait_ge(sq_summed, 1)
            nc.tensor.matmul(out_bank[2][:, 0:1], mean_of[:, :], sq_sum[:, :],
                             start=True, stop=True).then_inc(sqmean_done, 1)

        @block.scalar
        def _(act):
            def relu_blocks(net, layer, blocks, dest, bias):
                for n, (o, ch) in enumerate(blocks):
                    act.wait_ge(mm_done[net, layer], n + 1)
                    nc.scalar.activation(dest[:, o, ch * CHUNK:(ch + 1) * CHUNK], out_bank[n % len(out_bank)],
                                         ACT.Relu, bias=bias[:, o:o + 1]).then_inc(relu_done[net, layer], 1)

            def std(net, layer):
                act.wait_ge(var_ready[net, layer], 1)
                w = layer_width(net, layer)
                nc.scalar.activation(norm[net, layer][:, 1, 0:w], norm[net, layer][:, 0, 0:w],
                                     ACT.Sqrt).then_inc(std_ready[net, layer], 1)

            def layer1(net):
                std(net, 0)
                act.wait_ge(coef_ready[net, 0], 1)
                for k in range(K0 // 2, K0):
                    last = nc.scalar.activation(w1_scaled[:, k, :], w1_sb[net][:, k, :], ACT.Copy,
                                                scale=norm[net, 0][:, 8, k:k + 1])
                last.then_inc(scaled_a[net, 0], 1)
                act.wait_ge(bias_ready[net, 0], 1)
                relu_blocks(net, 1, [(o, ch) for ch in range(CHUNKS) for o in range(K1)], hidden1, bias1[net])

            act.wait_ge(bottom_loaded, 48)
            relu_blocks("bot", 0, [(o, ch) for ch in range(CHUNKS) for o in range(K0)], hidden0,
                        p_col("bot", "b", 0))
            act.wait_ge(bw1_loaded, 48)
            layer1("bot")
            std("bot", 1)
            act.wait_ge(bias_ready["bot", 1], 1)
            relu_blocks("bot", 2, [(0, ch) for ch in range(CHUNKS)], x_raw[:, :].rearrange("p (a b) -> p a b", a=1),
                        bias2["bot"])
            std("bot", 2)
            act.wait_ge(coef_ready["bot", 2], 1)
            nc.scalar.activation(x_all[:, :], x_raw[:, :], ACT.Identity, scale=norm["bot", 2][:, 8, 0:1],
                                 bias=norm["bot", 2][:, 9, 0:1]).then_inc(x_ready, 1)

            act.wait_ge(x_ready, 1)
            act.wait_ge(cleared, 1)
            with act.Fori(0, PAIRS // 2) as it:
                for s in range(2):
                    i = it * 2 + s
                    for h in range(2):
                        rows = slice(h * D, (h + 1) * D)
                        last = nc.scalar.activation(TT[rows, s, :, NF:V].rearrange("p b v -> p (b v)"),
                                                    x_all[rows, bass.ds(i * (2 * P) + h * P, P)], ACT.Copy)
                    last.then_inc(tt_x_written, 1)
                    for r in range(ROUNDS):
                        act.wait_ge(z_done, i * ROUNDS + (r + 1))
                        last = take_blocks(act_copy, r, (2, 3))
                        last.then_inc(z_taken_a, 1)
                    for o in range(K0):
                        act.wait_ge(l0_done, i * K0 + (o + 1))
                        nc.scalar.activation(hidden0[:, o, bass.ds(i * (2 * P), 2 * P)], acc_bank[o][:, 0:2 * P],
                                             ACT.Relu, bias=p_col("top", "b", 0)[:, o:o + 1]).then_inc(l0_relu, 1)

            act.wait_ge(top_loaded, 48)
            layer1("top")
            std("top", 1)
            act.wait_ge(logits_done, 1)
            act.wait_ge(bias_ready["top", 1], 1)
            nc.scalar.activation(logits[:, :], out_bank[0], ACT.Relu, bias=bias2["top"][:, :],
                                 accum_out=logit_sum[:, :]).then_inc(logit_summed, 1)
            act.wait_ge(logit_summed, 1)
            act.wait_ge(mean_ready, 1)
            nc.scalar.activation(logit_sq[:, :], logits[:, :], ACT.Square, bias=neg_mean[:, :],
                                 accum_out=sq_sum[:, :]).then_inc(sq_summed, 1)
            std("top", 2)
            act.wait_ge(coef_ready["top", 2], 1)
            nc.scalar.activation(prob[:, :, :].rearrange("p b u -> p u b"),
                                 logits[:, :].rearrange("p (u b) -> p u b", u=CT), ACT.Sigmoid,
                                 scale=norm["top", 2][:, 8, 0:1],
                                 bias=norm["top", 2][:, 9, 0:1]).then_inc(prob_ready, 1)

        @block.vector
        def _(dve):
            def chain(semaphore, count):
                done = [count]

                def step(ins):
                    done[0] += 1
                    ins.then_inc(semaphore, 1)
                    dve.wait_ge(semaphore, done[0])
                return step

            def block_stats(net, layer, blocks, src):
                for n, (o, ch) in enumerate(blocks):
                    dve.wait_ge(relu_done[net, layer], n + 1)
                    last = nc.vector.bn_stats(stats[net, layer][:, o, ch, :],
                                              src[:, o, ch * CHUNK:(ch + 1) * CHUNK])
                last.then_inc(stats_done[net, layer], 1)
                dve.wait_ge(stats_done[net, layer], 1)

            def scale_of(net, layer, step):
                v = norm[net, layer]
                w = layer_width(net, layer)
                dve.wait_ge(std_ready[net, layer], 1)
                step(nc.vector.reciprocal(v[:, 2, 0:w], v[:, 1, 0:w]))
                nc.vector.tensor_tensor(v[:, 3, 0:w], v[:, 2, 0:w], p_col(net, "g", layer), ALU.mult)
                step(nc.vector.tensor_tensor(v[:, 4, 0:w], v[:, 2, 0:w], v[:, 2, 0:w], ALU.mult))
                step(nc.vector.scalar_tensor_tensor(out=v[:, 5, 0:w], in0=v[:, 4, 0:w], scalar=-0.5,
                                                    in1=v[:, 0, 0:w], op0=ALU.mult, op1=ALU.mult))
                step(nc.vector.scalar_tensor_tensor(out=v[:, 8, 0:w], in0=v[:, 5, 0:w], scalar=1.5,
                                                    in1=v[:, 3, 0:w], op0=ALU.add, op1=ALU.mult))

            def coefficients(net, layer):
                v = norm[net, layer]
                w = layer_width(net, layer)
                step = chain(bn_step[net, layer], 0)
                for k in range(w):
                    last = nc.vector.bn_aggr(moments[net, layer][:, k, :],
                                             stats[net, layer][:, k, :, :].rearrange("p a b -> p (a b)"))
                step(last)
                mean, var = moments[net, layer][:, 0:w, 0], moments[net, layer][:, 0:w, 1]
                nc.vector.tensor_scalar_add(v[:, 0, 0:w], var, EPS).then_inc(var_ready[net, layer], 1)
                scale_of(net, layer, step)
                step(nc.vector.tensor_tensor(v[:, 7, 0:w], v[:, 8, 0:w], mean, ALU.mult))
                nc.vector.tensor_tensor(v[:, 9, 0:w], p_col(net, "beta", layer), v[:, 7, 0:w],
                                        ALU.subtract).then_inc(coef_ready[net, layer], 1)

            def layer1(net):
                coefficients(net, 0)
                for k in range(K0 // 2):
                    last = nc.vector.tensor_scalar_mul(w1_scaled[:, k, :], w1_sb[net][:, k, :],
                                                       norm[net, 0][:, 8, k:k + 1])
                last.then_inc(scaled_v[net, 0], 1)
                dve.wait_ge(fold_done[net, 0], 1)
                nc.vector.tensor_tensor(bias1[net][:, :], small[:, 0:K1], p_col(net, "b", 1),
                                        ALU.add).then_inc(bias_ready[net, 0], 1)
                block_stats(net, 1, [(o, ch) for ch in range(CHUNKS) for o in range(K1)], hidden1)

            def make_rows(step, cols):
                step(nc.vector.tensor_scalar(idx_neg[:, cols], idx_raw[:, cols], 0.0, float(VOCAB),
                                             ALU.is_lt, ALU.mult))
                step(nc.vector.tensor_tensor(idx_wrapped[:, cols], idx_raw[:, cols], idx_neg[:, cols], ALU.add))
                step(nc.vector.tensor_scalar(idx_clamped[:, cols], idx_wrapped[:, cols], 0.0, float(VOCAB - 1),
                                             ALU.max, ALU.min))
                step(nc.vector.tensor_tensor(idx_row[:, cols], idx_clamped[:, cols], table_base[:, cols], ALU.add))

            dve.wait_ge(idx_loaded, 16)
            dve.wait_ge(base_ready, 2)
            step = chain(idx_step, 0)
            for cols in (slice(0, PW), slice(PW, 2 * PW)):
                make_rows(step, cols)
                nc.vector.tensor_copy(stage[:, cols.start // PW, :], idx_row[:, cols]).then_inc(slot_open, 1)
            make_rows(step, slice(2 * PW, PAIRS * PW))
            nc.vector.memset(Zs[:, :, :], 0.0).then_inc(cleared, 1)
            nc.vector.memset(idx_row[:, PAIRS * PW:(PAIRS + 2) * PW], 0).then_inc(consts_ready, 1)
            nc.vector.memset(ones[:, :], 1.0).then_inc(consts_ready, 1)
            nc.vector.memset(mean_of[:, :], 1.0 / (QUAD * B)).then_inc(consts_ready, 1)
            dve.wait_ge(consts_ready, 3)

            dve.wait_ge(bottom_loaded, 48)
            block_stats("bot", 0, [(o, ch) for ch in range(CHUNKS) for o in range(K0)], hidden0)
            dve.wait_ge(bw1_loaded, 48)
            layer1("bot")
            coefficients("bot", 1)
            for k in range(K1):
                last = nc.vector.tensor_scalar_mul(w2_scaled[:, k, :], bw2_sb[:, k, :], norm["bot", 1][:, 8, k:k + 1])
            last.then_inc(scaled_v["bot", 1], 1)
            dve.wait_ge(fold_done["bot", 1], 1)
            nc.vector.tensor_tensor(bias2["bot"][:, :], small[:, 0:1], p_col("bot", "b", 2),
                                    ALU.add).then_inc(bias_ready["bot", 1], 1)
            block_stats("bot", 2, [(0, ch) for ch in range(CHUNKS)], x_raw[:, :].rearrange("p (a b) -> p a b", a=1))
            coefficients("bot", 2)

            dve.wait_ge(cleared, 1)
            with dve.Fori(0, PAIRS // 2) as it:
                for s in range(2):
                    i = it * 2 + s
                    for a in range(PARTS):
                        for g in range(GROUPS):
                            n = a * GROUPS + g
                            n0, w = 2 * group_pairs(g)[0], 2 * len(group_pairs(g))
                            dve.wait_ge(transposed, i * (PARTS * GROUPS) + (n + 1))
                            nc.vector.tensor_copy(
                                TT[:, s, a * PART:(a + 1) * PART, n0:n0 + w].rearrange("p b n -> p n b"),
                                tr_bank[n % 2][:, 0:w * PART].rearrange("p (n b) -> p n b", n=w),
                            ).then_inc(tt_written, 1)
                        if a == PARTS - 1:
                            nc.vector.tensor_copy(stage[:, s, :],
                                                  idx_row[:, bass.ds((i + 2) * PW, PW)]).then_inc(slot_open, 1)
                        for r in (2 * a, 2 * a + 1):
                            dve.wait_ge(z_done, i * ROUNDS + (r + 1))
                            last = take_blocks(nc.vector.tensor_copy, r, (0, 1))
                            last.then_inc(z_taken_v, 1)
                    for o in range(K0):
                        dve.wait_ge(l0_relu, i * K0 + (o + 1))
                        nc.vector.bn_stats(stats["top", 0][:, o, bass.ds(i, 1), :].rearrange("p a b -> p (a b)"),
                                           hidden0[:, o, bass.ds(i * (2 * P), 2 * P)]).then_inc(top0_stats, 1)

            dve.wait_ge(top0_stats, PAIRS * K0)
            layer1("top")
            coefficients("top", 1)
            dve.wait_ge(coef_ready["top", 1], 1)
            nc.vector.tensor_tensor(shift_w2[:, :], norm["top", 1][:, 9, 0:K1], p_col("top", "W", 2),
                                    ALU.mult).then_inc(scaled_v["top", 1], 1)
            for k in range(K1):
                last = nc.vector.tensor_scalar(tw2_rep[:, k, :], ones[:, 0:QUAD], p_col("top", "W", 2)[:, k:k + 1],
                                               norm["top", 1][:, 8, k:k + 1], ALU.mult, ALU.mult)
            last.then_inc(scaled_v["top", 1], 1)
            dve.wait_ge(fold_done["top", 1], 1)
            nc.vector.tensor_tensor(bias2["top"][:, :], small[:, 8:9], p_col("top", "b", 2),
                                    ALU.add).then_inc(bias_ready["top", 1], 1)
            dve.wait_ge(mean_done, 1)
            nc.vector.tensor_scalar_mul(neg_mean[:, :], out_bank[1][:, 0:1], -1.0).then_inc(mean_ready, 1)
            dve.wait_ge(sqmean_done, 1)
            v = norm["top", 2]
            nc.vector.tensor_scalar_add(v[:, 0, 0:1], out_bank[2][:, 0:1], EPS).then_inc(var_ready["top", 2], 1)
            scale_of("top", 2, chain(bn_step["top", 2], 0))
            nc.vector.tensor_scalar(v[:, 9, 0:1], neg_mean[:, :], v[:, 8, 0:1], p_col("top", "beta", 2),
                                    ALU.mult, ALU.add).then_inc(coef_ready["top", 2], 1)


def kernel(**inputs):
    import numpy as np
    import concourse.bacc as bacc
    from concourse import mybir as mb
    from concourse.bass_utils import run_bass_kernel_spmd as run

    def get(name):
        return np.ascontiguousarray(inputs[name])

    def columns(vec):
        return vec.reshape(-1, P).T

    dense_t = get("r_dense_inputs").reshape(CHUNKS, P, CT, DENSE).transpose(3, 0, 2, 1).reshape(DENSE, B)
    idx = get("r_sparse_inputs").reshape(CHUNKS, PARTS, PART, CT // 2, 2, TP, 2)
    idx = idx.transpose(6, 2, 0, 3, 1, 5, 4).reshape(P, TILES * NF)
    params = np.zeros((P, NPARAM), np.float32)
    for (net, what, layer), (at, width) in PARAMS.items():
        vec = get("L0_rec_%s_%s%d" % (net, what, layer)).reshape(-1)
        if vec.size < P:
            vec = np.tile(vec, P // vec.size)
        params[:, at:at + width] = columns(vec)
    w0 = get("L0_rec_top_W0")
    twx = np.zeros((P, H0), np.float32)
    twx[0:D] = w0[0:D]
    tw0x = np.zeros((P, ZC, H0), np.float32)
    for row, (n, m) in enumerate(zip(*np.triu_indices(V, k=1))):
        q, c = divmod(m - 1, ZC)
        tw0x[QUAD * q + n, c] = w0[D + row]

    arrays = {
        "idx": np.ascontiguousarray(idx),
        "table": get("L0_rec_emb_tables").reshape(NF * VOCAB, D),
        "dense_t": np.ascontiguousarray(dense_t),
        "params": params,
        "identity": np.eye(P, dtype=np.float32),
        "bw0": get("L0_rec_bot_W0"), "bw1": get("L0_rec_bot_W1"), "bw2": get("L0_rec_bot_W2"),
        "tw0x": tw0x, "twx": twx, "tw1": get("L0_rec_top_W1"),
    }
    nc = bacc.Bacc("TRN2", target_bir_lowering=False, num_devices=1)
    args = [nc.dram_tensor(k, a.shape, mb.dt.from_np(a.dtype), kind="ExternalInput").ap() for k, a in arrays.items()]
    out = nc.dram_tensor("out", (CHUNKS, CHUNK), mb.dt.float32, kind="ExternalOutput").ap()
    rec_program(nc, *args, out)
    result = run(nc, [arrays], core_ids=[0])
    return result.results[0]["out"].reshape(B, 1)
```

```python
from contextlib import ExitStack

import concourse.bass as bass
from concourse import mybir

F32 = mybir.dt.float32
F32R = mybir.dt.float32r
I32 = mybir.dt.int32
U32 = mybir.dt.uint32
ALU = mybir.AluOpType
ACT = mybir.ActivationFunctionType

P = 128
B = 2048
NF = 26
V = NF + 1
D = 64
VOCAB = 12500
DENSE = 13
H0, H1 = 512, 256
K0, K1 = H0 // P, H1 // P
EPS = 1e-5

QUAD = 32
NQ = P // QUAD
ZC = 7
UNIT = P // 2
PARTS = B // (2 * UNIT)
SLOTS = 3
LOOPS = (PARTS - 1) // SLOTS
LAST = PARTS - 1
LAST_SLOT = LAST % SLOTS
LAST_GROUPS = ((0, 8), (8, 12), (12, 13))
HALF = H0 // 2
TP = NF // 2
GROUP = 4
GROUPS = -(-TP // GROUP)
RX = UNIT // NQ
ZM = NF
CHUNK = 512
CHUNKS = B // CHUNK
CU = CHUNK // UNIT
PW = NF
FIRST_COLS = slice(0, SLOTS * PW)
LATER_COLS = slice(SLOTS * PW, PARTS * PW)

PARAMS = {}
for _net in ("bot", "top"):
    for _layer, _w in ((0, K0), (1, K1), (2, 1)):
        for _what in ("b", "g", "beta"):
            PARAMS[_net, _what, _layer] = (sum(w for _, w in PARAMS.values()), _w)
PARAMS["top", "W", 2] = (sum(w for _, w in PARAMS.values()), K1)
NPARAM = sum(w for _, w in PARAMS.values())


def group_pairs(g):
    return range(g * GROUP, min((g + 1) * GROUP, TP))


def quadrant_columns(q):
    return min(ZC, NF - ZC * q)


def rec_program(nc, idx, table, dense_t, params, identity, bw0, bw1, bw2, tw0x, twx, tw1, out):
    ctx = ExitStack()
    with ctx:
        def sb(name, shape, dt=F32):
            return ctx.enter_context(nc.sbuf_tensor(name, shape, dt))

        def ps(name, shape):
            return ctx.enter_context(nc.psum_tensor(name, shape, F32))

        def sem(name):
            return ctx.enter_context(nc.semaphore(name))

        idx_raw = sb("idx_raw", [P, PARTS * PW], I32)
        idx_neg = sb("idx_neg", [P, PARTS * PW])
        idx_wrapped = sb("idx_wrapped", [P, PARTS * PW])
        idx_clamped = sb("idx_clamped", [P, (PARTS + SLOTS) * PW])
        table_base = sb("table_base", [P, PW], I32)
        stage = sb("stage", [P, SLOTS, PW], U32)
        emb = sb("emb", [P, SLOTS, TP, 2, D])
        emb_last = emb[:, LAST_SLOT, :, :, :].rearrange("p k h d -> p (k h d)").rearrange(
            "p (h k d) -> p h k d", h=2, k=TP)
        TT = sb("TT", [P, 2, UNIT, V])
        Zs = sb("Zs", [P, ZC, 2 * UNIT])
        pre0 = sb("pre0", [P, 2, HALF])
        x_all = sb("x_all", [P, B])
        h0_block = sb("h0_block", [P, 2, CHUNK])
        h0_part = h0_block[:, 0, :].rearrange("p (k b) -> p k b", k=K0)
        hidden0 = {"hi": sb("hidden0_hi", [P, K0, B], F32R), "lo": sb("hidden0_lo", [P, K0, B], F32R)}
        hidden1 = sb("hidden1", [P, K1, B])
        dense_sb = hidden1[0:DENSE, 0, :]
        par = sb("par", [P, NPARAM])
        ident = sb("ident", [P, P])
        bw0_sb = sb("bw0_sb", [DENSE, H0])
        w1_sb = {"bot": sb("bw1_sb", [P, K0, H1]), "top": sb("tw1_sb", [P, K0, H1])}
        w1_scaled = {"hi": sb("w1_hi", [P, K0, H1], F32R), "lo": sb("w1_lo", [P, K0, H1], F32R)}
        bw2_sb = sb("bw2_sb", [P, K1, 2 * D])
        w2_scaled = sb("w2_scaled", [P, K1, 2 * D])
        tw0_sb = sb("tw0_sb", [P, ZC, H0])
        twx_sb = sb("twx_sb", [P, H0])
        stats = {("bot", 0): sb("stats_b0", [P, K0, CHUNKS, 6]), ("bot", 1): sb("stats_b1", [P, K1, CHUNKS, 6]),
                 ("bot", 2): sb("stats_b2", [P, 1, CHUNKS, 6]), ("top", 0): sb("stats_t0", [P, K0, PARTS, 6]),
                 ("top", 1): sb("stats_t1", [P, K1, CHUNKS, 6])}
        norm = {key: sb("norm_%s%d" % key, [P, 10, K0]) for key in
                [(n, l) for n in ("bot", "top") for l in range(3)]}
        moments = {key: sb("moments_%s%d" % key, [P, K0, 2]) for key in stats}
        bias1 = {"bot": sb("bias1_bot", [P, K1]), "top": sb("bias1_top", [P, K1])}
        bias2 = {"bot": sb("bias2_bot", [P, 1]), "top": sb("bias2_top", [P, 1])}
        shift_w1 = sb("shift_w1", [P, H1])
        shift_w2 = sb("shift_w2", [P, K1])
        tw2_rep = sb("tw2_rep", [P, K1, QUAD])
        ones = sb("ones", [P, P])
        idle_operand = sb("idle_operand", [P, CHUNK], mybir.dt.bfloat16)
        eps_col = sb("eps_col", [P, 1])
        mean_of = sb("mean_of", [P, P])
        logits = sb("logits", [P, CHUNK])
        logit_sum = sb("logit_sum", [P, 1])
        neg_mean = sb("neg_mean", [P, 1])
        logit_sq = sb("logit_sq", [P, CHUNK])
        sq_sum = sb("sq_sum", [P, 1])
        prob = sb("prob", [P, UNIT, CU])

        tr_bank = [ps("tr_bank%d" % k, [P, GROUP * P]) for k in range(2)]
        z_bank = [ps("z_bank%d" % k, [P, 512]) for k in range(2)]
        l0_bank = [ps("l0_bank%d" % k, [P, 512]) for k in range(K0)]
        last_tr_bank = [tr_bank[0], tr_bank[1], z_bank[1]]
        out_bank = [bank[:, :] for bank in l0_bank]
        small = tr_bank[1]

        first_idx_loaded = sem("first_idx_loaded")
        idx_loaded = sem("idx_loaded")
        bottom_loaded = sem("bottom_loaded")
        bw1_loaded = sem("bw1_loaded")
        ident_loaded = sem("ident_loaded")
        top_loaded = sem("top_loaded")
        base_ready = sem("base_ready")
        idx_step = sem("idx_step")
        cleared = sem("cleared")
        consts_ready = sem("consts_ready")
        slot_open = sem("slot_open")
        part_started = sem("part_started")
        landed = [[sem("landed%d_%d" % (s, g)) for g in range(GROUPS)] for s in range(SLOTS)]
        landed_last = [[sem("landed_last%d_%d" % (h, g)) for g in range(len(LAST_GROUPS))] for h in range(2)]
        transposed = sem("transposed")
        tt_written = sem("tt_written")
        tt_x_written = sem("tt_x_written")
        z_started = sem("z_started")
        z_done = sem("z_done")
        z_taken_v = sem("z_taken_v")
        z_taken_a = sem("z_taken_a")
        l0_done = sem("l0_done")
        l0_relu = sem("l0_relu")
        top0_stats = sem("top0_stats")
        h0_hi = sem("h0_hi")
        h0_f32 = sem("h0_f32")
        h0_lo = {net: sem("h0_lo_" + net) for net in ("bot", "top")}
        w1_lo = {net: sem("w1_lo_" + net) for net in ("bot", "top")}
        shift_summed = {net: sem("shift_summed_" + net) for net in ("bot", "top")}
        last_transposed = sem("last_transposed")
        last_tt_v = sem("last_tt_v")
        last_tt_a = sem("last_tt_a")
        last_z_done = sem("last_z_done")
        last_taken_v = sem("last_taken_v")
        last_taken_a = sem("last_taken_a")
        last_l0 = sem("last_l0")
        pre0_a = sem("pre0_a")
        pre0_v = sem("pre0_v")
        last_backs = sem("last_backs")
        last_hi = sem("last_hi")
        last_lo = sem("last_lo")
        last_relu_a = sem("last_relu_a")
        last_relu_v = sem("last_relu_v")
        mm_done = {k: sem("mm_done_%s%d" % k) for k in (("bot", 0), ("bot", 1), ("bot", 2), ("top", 1))}
        relu_done = {k: sem("relu_done_%s%d" % k) for k in mm_done}
        stats_done = {k: sem("stats_done_%s%d" % k) for k in mm_done}
        bn_step = {k: sem("bn_step_%s%d" % k) for k in norm}
        scale_ready = {k: sem("scale_ready_%s%d" % k) for k in norm}
        std_ready = {k: sem("std_ready_%s%d" % k) for k in norm}
        coef_ready = {k: sem("coef_ready_%s%d" % k) for k in norm}
        scaled_v = {k: sem("scaled_v_%s%d" % k) for k in (("bot", 0), ("bot", 1), ("top", 0), ("top", 1))}
        scaled_a = {k: sem("scaled_a_%s%d" % k) for k in (("bot", 0), ("top", 0))}
        fold_done = {k: sem("fold_done_%s%d" % k) for k in scaled_v}
        bias_ready = {k: sem("bias_ready_%s%d" % k) for k in scaled_v}
        x_ready = sem("x_ready")
        logits_done = sem("logits_done")
        logit_summed = sem("logit_summed")
        mean_ready = sem("mean_ready")
        sq_summed = sem("sq_summed")
        mean_done = sem("mean_done")
        sqmean_done = sem("sqmean_done")
        prob_ready = sem("prob_ready")
        stored = sem("stored")

        def p_col(net, what, layer):
            at, width = PARAMS[net, what, layer]
            return par[:, at:at + width]

        def layer_width(net, layer):
            return PARAMS[net, "b", layer][1]

        def take_z(copy, bank, h, quadrants, x0=0, x1=RX):
            for j in quadrants:
                src = bank[QUAD * j:QUAD * j + V, x0 * ZM:x1 * ZM].rearrange("p (x c) -> p x c", c=ZM)
                for q in range(NQ):
                    w = quadrant_columns(q)
                    dst = Zs[QUAD * q:QUAD * q + V, 0:w, :].rearrange(
                        "p c (h x j) -> p h x j c", h=2, j=NQ)[:, h, x0:x1, j, :]
                    last = copy(dst, src[:, :, ZC * q:ZC * q + w])
            return last

        def last_blocks(g):
            k0, k1 = LAST_GROUPS[g]
            return [(k, min(k + 2, k1)) for k in range(k0, k1, 2)]

        def last_tt(copy, h, g, f):
            nb, n0 = len(last_blocks(g)), 2 * LAST_GROUPS[g][0]
            src = last_tr_bank[g][f * D:(f + 1) * D, 0:nb * P].rearrange("p (j e b) -> p j e b", j=nb, e=2)
            if g == len(LAST_GROUPS) - 1:
                return copy(TT[0:D, h, :, n0:n0 + 2].rearrange("p b e -> p e b"), src[:, 0, :, :])
            dst = TT[0:D, h, :, n0:n0 + 4 * nb].rearrange("p b (j n) -> p j n b", n=4)
            return copy(dst[:, :, 2 * f:2 * f + 2, :], src)

        def upper_copies(n):
            return n - n // len(LAST_GROUPS)

        def last_columns(h):
            return slice(LAST * 2 * UNIT + h * UNIT, LAST * 2 * UNIT + (h + 1) * UNIT)

        def act_copy(dst, src):
            return nc.scalar.activation(dst, src, ACT.Copy)

        block = ctx.enter_context(nc.Block())

        @block.sync
        def _(sp):
            sp.dma_start(idx_raw[:, FIRST_COLS], idx[:, FIRST_COLS]).then_inc(first_idx_loaded, 16)
            sp.dma_start(idx_raw[:, LATER_COLS], idx[:, LATER_COLS]).then_inc(idx_loaded, 16)
            sp.dma_start(dense_sb[:, :], dense_t).then_inc(bottom_loaded, 16)
            sp.dma_start(bw0_sb[:, :], bw0).then_inc(bottom_loaded, 16)
            sp.dma_start(par[:, :], params).then_inc(bottom_loaded, 16)
            sp.dma_start(w1_sb["bot"][:, :, :], bw1.rearrange("(k p) n -> p k n", p=P)).then_inc(bw1_loaded, 16)
            for dup in range(2):
                sp.dma_start(bw2_sb[:, :, dup * D:(dup + 1) * D],
                             bw2.rearrange("(k p) n -> p k n", p=P)).then_inc(bw1_loaded, 16)
            sp.dma_start(ident[:, :], identity).then_inc(ident_loaded, 16)
            sp.dma_start(tw0_sb[:, :, :], tw0x).then_inc(top_loaded, 16)
            sp.dma_start(twx_sb[:, :], twx).then_inc(top_loaded, 16)
            sp.dma_start(w1_sb["top"][:, :, :], tw1.rearrange("(k p) n -> p k n", p=P)).then_inc(top_loaded, 16)
            sp.wait_ge(prob_ready, 1)
            sp.dma_start(out, prob[0:P:QUAD, :, :].rearrange("p a b -> p (a b)")).then_inc(stored, 16)
            sp.wait_ge(stored, 16)

        @block.gpsimd
        def _(pool):
            for e in range(2):
                pool.iota(table_base[e * UNIT:(e + 1) * UNIT, :], pattern=[[2 * VOCAB, TP], [0, 2]],
                          base=e * VOCAB, channel_multiplier=0).then_inc(base_ready, 1)
            with pool.Fori(0, LOOPS) as it:
                for s in range(SLOTS):
                    pool.wait_ge(slot_open, it * SLOTS + (s + 1))
                    pool.sem_inc(part_started, 1)
                    for k in range(TP):
                        for h in range(2):
                            col = 2 * k + h
                            pool.indirect_dma_start(
                                out=emb[:, s, k, h, :], out_offset=None, in_=table,
                                in_offset=bass.IndirectOffsetOnAxis(ap=stage[:, s, col:col + 1], axis=0),
                            ).then_inc(landed[s][k // GROUP], 16)
            pool.wait_ge(slot_open, PARTS)
            pool.sem_inc(part_started, 1)
            for h in range(2):
                for g, (k0, k1) in enumerate(LAST_GROUPS):
                    for k in range(k0, k1):
                        col = 2 * k + h
                        pool.indirect_dma_start(
                            out=emb_last[:, h, k, :], out_offset=None, in_=table,
                            in_offset=bass.IndirectOffsetOnAxis(ap=stage[:, LAST_SLOT, col:col + 1], axis=0),
                        ).then_inc(landed_last[h][g], 16)

            for n, o in enumerate((0, 2, 1, 3)):
                pool.wait_ge(last_hi, n + 1)
                part = slice(LAST * 2 * UNIT, B)
                pool.tensor_tensor(hidden0["lo"][:, o, part], h0_part[:, o, :], hidden0["hi"][:, o, part],
                                   ALU.subtract).then_inc(last_lo, 1)

        @block.tensor
        def _(pe):
            def keep_clock(n, bank):
                for _ in range(n):
                    nc.tensor.matmul(bank[:, :], idle_operand[:, 0:P], idle_operand[:, :], start=True, stop=True)

            def layer_out(net, layer, k):
                if k >= len(out_bank):
                    pe.wait_ge(relu_done[net, layer], k - len(out_bank) + 1)
                return out_bank[k % len(out_bank)]

            def fold_shift(net, weights, layer, width):
                pe.wait_ge(coef_ready[net, layer], 1)
                shift = norm[net, layer][:, 9, :]
                kn = layer_width(net, layer)
                for o in range(width):
                    for k in range(kn):
                        mm = nc.tensor.matmul(small[:, o:o + 1], weights[:, k, o * P:(o + 1) * P],
                                              shift[:, k:k + 1], start=(k == 0), stop=(k == kn - 1))
                mm.then_inc(fold_done[net, layer], 1)

            def layer1(net):
                order = [(0, scaled_v, 1), (2, scaled_a, 1), (1, scaled_v, 2), (3, scaled_a, 2)]
                pe.wait_ge(h0_lo[net], CHUNKS * K0 if net == "bot" else LAST * K0)
                if net == "top":
                    pe.wait_ge(last_lo, K0)
                for ch in range(CHUNKS):
                    if ch == 1:
                        pe.wait_ge(shift_summed[net], K0)
                        for o in range(K1):
                            fold = nc.tensor.matmul(small[:, o:o + 1], shift_w1[:, o * P:(o + 1) * P],
                                                    ones[:, 0:1], start=True, stop=True)
                        fold.then_inc(fold_done[net, 0], 1)
                    for o in range(K1):
                        bank = layer_out(net, 1, ch * K1 + o)
                        for n, (k, scaled, count) in enumerate(order):
                            if ch == 0 and o == 0:
                                pe.wait_ge(scaled[net, 0], count)
                            for part in ("hi", "lo"):
                                nc.tensor.matmul(bank, w1_scaled["hi"][:, k, o * P:(o + 1) * P],
                                                 hidden0[part][:, k, ch * CHUNK:(ch + 1) * CHUNK],
                                                 start=(n == 0 and part == "hi"), stop=False)
                        for n, (k, _, _) in enumerate(order):
                            if ch == 0 and o == 0:
                                pe.wait_ge(w1_lo[net], n + 1)
                            mm = nc.tensor.matmul(bank, w1_scaled["lo"][:, k, o * P:(o + 1) * P],
                                                  hidden0["hi"][:, k, ch * CHUNK:(ch + 1) * CHUNK],
                                                  start=False, stop=(n == K0 - 1))
                        mm.then_inc(mm_done[net, 1], 1)

            pe.wait_ge(bottom_loaded, 48)
            for ch in range(CHUNKS):
                for o in range(K0):
                    bank = layer_out("bot", 0, ch * K0 + o)
                    nc.tensor.matmul(bank, bw0_sb[:, o * P:(o + 1) * P], dense_sb[:, ch * CHUNK:(ch + 1) * CHUNK],
                                     start=True, stop=True).then_inc(mm_done["bot", 0], 1)
            pe.wait_ge(bw1_loaded, 48)
            pe.wait_ge(relu_done["bot", 0], CHUNKS * K0)
            layer1("bot")
            pe.wait_ge(bias_ready["bot", 0], 1)
            fold_shift("bot", bw2_sb, 1, 1)
            pe.wait_ge(scaled_v["bot", 1], 1)
            pe.wait_ge(relu_done["bot", 1], CHUNKS * K1)
            for ch in range(CHUNKS):
                bank = layer_out("bot", 2, ch)
                for k in range(K1):
                    mm = nc.tensor.matmul(bank, w2_scaled[:, k, :], hidden1[:, k, ch * CHUNK:(ch + 1) * CHUNK],
                                          start=(k == 0), stop=(k == K1 - 1))
                mm.then_inc(mm_done["bot", 2], 1)

            pe.wait_ge(bias_ready["bot", 1], 1)
            pe.wait_ge(ident_loaded, 16)
            pe.wait_ge(top_loaded, 48)
            pe.wait_ge(cleared, 1)
            with pe.Fori(0, LOOPS) as it:
                for s in range(SLOTS):
                    i = it * SLOTS + s
                    for g in range(GROUPS):
                        pairs = group_pairs(g)
                        pe.wait_ge(landed[s][g], (it + 1) * (len(pairs) * 2 * 16))
                        if g >= 2:
                            pe.wait_ge(tt_written, i * GROUPS + (g - 1))
                        for c, k in enumerate(pairs):
                            tr = nc.tensor.transpose(tr_bank[g % 2][:, c * P:(c + 1) * P],
                                                     emb[:, s, k, :, :].rearrange("p h d -> p (h d)"),
                                                     ident[:, :])
                        tr.then_inc(transposed, 1)
                    pe.wait_ge(tt_written, (i + 1) * GROUPS)
                    pe.wait_ge(tt_x_written, i + 1)
                    pe.sem_inc(z_started, 1)
                    for h in range(2):
                        bank = z_bank[h]
                        for x in range(RX):
                            for j in range(NQ):
                                one = TT[h * D:(h + 1) * D, 0, x * NQ + j, :]
                                mm = nc.tensor.matmul(bank[QUAD * j:QUAD * j + V, x * ZM:(x + 1) * ZM],
                                                      one, one[:, 1:V], start=True, stop=True)
                        mm.then_inc(z_done, 1)
                    keep_clock(7, tr_bank[0])
                    pe.wait_ge(z_taken_v, (i + 1) * 2)
                    pe.wait_ge(z_taken_a, (i + 1) * 2)
                    for o in range(K0):
                        acc = l0_bank[o][:, 0:2 * UNIT]
                        cols = slice(o * P, (o + 1) * P)
                        nc.tensor.matmul(acc, twx_sb[:, cols], x_all[:, bass.ds(i * (2 * UNIT), 2 * UNIT)],
                                         start=True, stop=False)
                        for c in range(ZC):
                            mm = nc.tensor.matmul(acc, tw0_sb[:, c, cols], Zs[:, c, :],
                                                  start=False, stop=(c == ZC - 1))
                        mm.then_inc(l0_done, 1)

            def last_transposes(h, g):
                pe.wait_ge(landed_last[h][g], (LAST_GROUPS[g][1] - LAST_GROUPS[g][0]) * 16)
                for c, (k, k_end) in enumerate(last_blocks(g)):
                    tr = nc.tensor.transpose(last_tr_bank[g][0:(k_end - k) * D, c * P:(c + 1) * P],
                                             emb_last[:, h, k:k_end, :].rearrange("p k d -> p (k d)"),
                                             ident[:, :])
                tr.then_inc(last_transposed, 1)

            def last_z(h):
                pe.wait_ge(last_tt_v, (h + 1) * len(LAST_GROUPS))
                pe.wait_ge(last_tt_a, upper_copies((h + 1) * len(LAST_GROUPS)))
                pe.wait_ge(tt_x_written, PARTS)
                for y in range(2):
                    for x in range(y * RX // 2, (y + 1) * RX // 2):
                        for j in range(NQ):
                            one = TT[0:D, h, x * NQ + j, :]
                            mm = nc.tensor.matmul(z_bank[y][QUAD * j:QUAD * j + V, x * ZM:(x + 1) * ZM],
                                                  one, one[:, 1:V], start=True, stop=True)
                    mm.then_inc(last_z_done, 1)

            def last_layer0(h, t, columns):
                for c in columns:
                    for f in range(2):
                        acc = l0_bank[t][f * UNIT:(f + 1) * UNIT, 0:P]
                        cols = slice(f * HALF + t * P, f * HALF + (t + 1) * P)
                        if c < 0:
                            mm = nc.tensor.matmul(acc, x_all[:, last_columns(h)], twx_sb[:, cols],
                                                  start=True, stop=False)
                        else:
                            mm = nc.tensor.matmul(acc, Zs[:, c, h * UNIT:(h + 1) * UNIT],
                                                  tw0_sb[:, c, cols], start=False, stop=(c == ZC - 1))
                return mm

            def last_back(h, t, copied, relu):
                pe.wait_ge(copied, h + 1)
                if h > 0:
                    pe.wait_ge(relu, h)
                nc.tensor.transpose(l0_bank[2 + t][:, 0:P], pre0[:, h, t * P:(t + 1) * P],
                                    ident[:, :]).then_inc(last_backs, 1)

            def last_layer0_with_back(h):
                pe.wait_ge(last_taken_v, (h + 1) * 2)
                pe.wait_ge(last_taken_a, (h + 1) * 2)
                last_layer0(h, 0, range(-1, ZC)).then_inc(last_l0, 1)
                last_layer0(h, 1, range(-1, 3))
                last_back(h, 0, pre0_a, last_relu_a)
                last_layer0(h, 1, range(3, ZC)).then_inc(last_l0, 1)

            for g in range(len(LAST_GROUPS)):
                last_transposes(0, g)
            keep_clock(7, z_bank[0])
            last_z(0)
            last_transposes(1, 0)
            keep_clock(2, tr_bank[1])
            pe.wait_ge(l0_relu, LAST * K0)
            last_layer0_with_back(0)
            last_transposes(1, 1)
            last_transposes(1, 2)
            last_back(0, 1, pre0_v, last_relu_v)
            keep_clock(1, z_bank[0])
            last_z(1)
            keep_clock(5, tr_bank[1])
            last_layer0_with_back(1)
            last_back(1, 1, pre0_v, last_relu_v)

            keep_clock(15, z_bank[0])
            layer1("top")
            keep_clock(16, z_bank[0])
            pe.wait_ge(scaled_v["top", 1], 1)
            pe.wait_ge(relu_done["top", 1], CHUNKS * K1)
            for k in range(K1):
                for j in range(CHUNKS):
                    mm = nc.tensor.matmul(out_bank[0][QUAD * j:QUAD * (j + 1), :], tw2_rep[:, k, :],
                                          hidden1[:, k, j * CHUNK:(j + 1) * CHUNK],
                                          start=(k == 0), stop=(k == K1 - 1))
                    if (k, j) == (0, CHUNKS - 1):
                        pe.wait_ge(scaled_v["top", 1], 2)
                        pe.wait_ge(bias_ready["top", 0], 1)
                        for kb in range(K1):
                            fold = nc.tensor.matmul(small[:, 8:9], ones[:, :], shift_w2[:, kb:kb + 1],
                                                    start=(kb == 0), stop=(kb == K1 - 1))
                        fold.then_inc(fold_done["top", 1], 1)
            mm.then_inc(logits_done, 1)
            keep_clock(3, z_bank[0])
            pe.wait_ge(logit_summed, 1)
            nc.tensor.matmul(out_bank[1][:, 0:1], mean_of[:, :], logit_sum[:, :],
                             start=True, stop=True).then_inc(mean_done, 1)
            pe.wait_ge(sq_summed, 1)
            nc.tensor.matmul(out_bank[2][:, 0:1], mean_of[:, :], sq_sum[:, :],
                             start=True, stop=True).then_inc(sqmean_done, 1)

        @block.scalar
        def _(act):
            def relu_blocks(net, layer, blocks, dest, bias):
                for n, (o, ch) in enumerate(blocks):
                    act.wait_ge(mm_done[net, layer], n + 1)
                    nc.scalar.activation(dest[:, o, ch * CHUNK:(ch + 1) * CHUNK], out_bank[n % len(out_bank)],
                                         ACT.Relu, bias=bias[:, o:o + 1]).then_inc(relu_done[net, layer], 1)

            def std(net, layer, var, ready, count):
                act.wait_ge(ready, count)
                nc.scalar.activation(norm[net, layer][:, 1, 0:layer_width(net, layer)], var, ACT.Sqrt,
                                     bias=eps_col[:, :]).then_inc(std_ready[net, layer], 1)

            def layer_std(net, layer):
                std(net, layer, moments[net, layer][:, 0:layer_width(net, layer), 1], bn_step[net, layer], 1)

            def layer1(net):
                layer_std(net, 0)
                act.wait_ge(scale_ready[net, 0], 1)
                for k in range(K0 // 2, K0):
                    nc.scalar.activation(w1_scaled["hi"][:, k, :], w1_sb[net][:, k, :], ACT.Copy,
                                         scale=norm[net, 0][:, 8, k:k + 1]).then_inc(scaled_a[net, 0], 1)
                act.wait_ge(bias_ready[net, 0], 1)
                relu_blocks(net, 1, [(o, ch) for ch in range(CHUNKS) for o in range(K1)], hidden1, bias1[net])

            act.wait_ge(bottom_loaded, 48)
            for n in range(CHUNKS * K0):
                ch, o = divmod(n, K0)
                bank, bias = out_bank[n % len(out_bank)], p_col("bot", "b", 0)[:, o:o + 1]
                act.wait_ge(mm_done["bot", 0], n + 1)
                nc.scalar.activation(hidden0["hi"][:, o, ch * CHUNK:(ch + 1) * CHUNK], bank, ACT.Relu,
                                     bias=bias).then_inc(h0_hi, 1)
                if n >= 2:
                    act.wait_ge(h0_lo["bot"], n - 1)
                nc.scalar.activation(h0_block[:, n % 2, :], bank, ACT.Relu,
                                     bias=bias).then_inc(relu_done["bot", 0], 1)
            act.wait_ge(bw1_loaded, 48)
            layer1("bot")
            layer_std("bot", 1)
            act.wait_ge(bias_ready["bot", 1], 1)
            relu_blocks("bot", 2, [(0, ch) for ch in range(CHUNKS)], x_all[:, :].rearrange("p (a b) -> p a b", a=1),
                        bias2["bot"])
            layer_std("bot", 2)
            act.wait_ge(coef_ready["bot", 2], 1)
            nc.scalar.activation(x_all[:, :], x_all[:, :], ACT.Identity, scale=norm["bot", 2][:, 8, 0:1],
                                 bias=norm["bot", 2][:, 9, 0:1]).then_inc(x_ready, 1)

            act.wait_ge(x_ready, 1)
            act.wait_ge(cleared, 1)
            with act.Fori(0, LOOPS) as it:
                for s in range(SLOTS):
                    i = it * SLOTS + s
                    for h in range(2):
                        half = slice(h * D, (h + 1) * D)
                        last = nc.scalar.activation(TT[half, 0, :, NF:V].rearrange("p b v -> p (b v)"),
                                                    x_all[half, bass.ds(i * (2 * UNIT) + h * UNIT, UNIT)],
                                                    ACT.Copy)
                    last.then_inc(tt_x_written, 1)
                    for h in range(2):
                        act.wait_ge(z_done, i * 2 + (h + 1))
                        take_z(act_copy, z_bank[h], h, (2, 3)).then_inc(z_taken_a, 1)
                    for o in range(K0):
                        act.wait_ge(l0_done, i * K0 + (o + 1))
                        nc.scalar.activation(h0_part[:, o, :], l0_bank[o][:, 0:2 * UNIT], ACT.Relu,
                                             bias=p_col("top", "b", 0)[:, o:o + 1]).then_inc(h0_f32, 1)
                        nc.scalar.activation(hidden0["hi"][:, o, bass.ds(i * (2 * UNIT), 2 * UNIT)],
                                             l0_bank[o][:, 0:2 * UNIT], ACT.Relu,
                                             bias=p_col("top", "b", 0)[:, o:o + 1]).then_inc(l0_relu, 1)

            for h in range(2):
                last = nc.scalar.activation(TT[0:D, h, :, NF:V].rearrange("p b v -> p (b v)"),
                                            x_all[0:D, last_columns(h)], ACT.Copy)
            last.then_inc(tt_x_written, 1)

            def last_upper(h, g):
                act.wait_ge(last_transposed, h * len(LAST_GROUPS) + g + 1)
                last_tt(act_copy, h, g, 1).then_inc(last_tt_a, 1)

            for h in range(2):
                for g in range(h, len(LAST_GROUPS) - 1):
                    last_upper(h, g)
                for y in range(2):
                    act.wait_ge(last_z_done, h * 2 + y + 1)
                    take_z(act_copy, z_bank[y], h, (2, 3), y * RX // 2, (y + 1) * RX // 2).then_inc(last_taken_a, 1)
                if h == 0:
                    last_upper(1, 0)
                act.wait_ge(last_l0, h * 2 + 1)
                nc.scalar.activation(pre0[:, h, 0:P], l0_bank[0][:, 0:P], ACT.Copy).then_inc(pre0_a, 1)
                act.wait_ge(last_backs, h * 2 + 1)
                for f in range(2):
                    last = nc.scalar.activation(h0_part[:, 2 * f, h * UNIT:(h + 1) * UNIT],
                                                l0_bank[2][:, f * UNIT:(f + 1) * UNIT], ACT.Relu,
                                                bias=p_col("top", "b", 0)[:, 2 * f:2 * f + 1])
                last.then_inc(last_relu_a, 1)
            for o, relu in ((0, last_relu_a), (2, last_relu_a), (1, last_relu_v), (3, last_relu_v)):
                act.wait_ge(relu, 2)
                nc.scalar.activation(hidden0["hi"][:, o, LAST * 2 * UNIT:B], h0_part[:, o, :],
                                     ACT.Copy).then_inc(last_hi, 1)

            act.wait_ge(top_loaded, 48)
            layer1("top")
            layer_std("top", 1)
            act.wait_ge(logits_done, 1)
            act.wait_ge(bias_ready["top", 1], 1)
            nc.scalar.activation(logits[:, :], out_bank[0], ACT.Relu, bias=bias2["top"][:, :],
                                 accum_out=logit_sum[:, :]).then_inc(logit_summed, 1)
            act.wait_ge(logit_summed, 1)
            act.wait_ge(mean_ready, 1)
            nc.scalar.activation(logit_sq[:, :], logits[:, :], ACT.Square, bias=neg_mean[:, :],
                                 accum_out=sq_sum[:, :]).then_inc(sq_summed, 1)
            std("top", 2, out_bank[2][:, 0:1], sqmean_done, 1)
            act.wait_ge(coef_ready["top", 2], 1)
            nc.scalar.activation(prob[:, :, :].rearrange("p b u -> p u b"),
                                 logits[:, :].rearrange("p (u b) -> p u b", u=CU), ACT.Sigmoid,
                                 scale=norm["top", 2][:, 8, 0:1],
                                 bias=norm["top", 2][:, 9, 0:1]).then_inc(prob_ready, 1)

        @block.vector
        def _(dve):
            def chain(semaphore, count):
                done = [count]

                def step(ins):
                    done[0] += 1
                    ins.then_inc(semaphore, 1)
                    dve.wait_ge(semaphore, done[0])
                return step

            def block_stats(net, layer, blocks, src):
                for n, (o, ch) in enumerate(blocks):
                    dve.wait_ge(relu_done[net, layer], n + 1)
                    last = nc.vector.bn_stats(stats[net, layer][:, o, ch, :],
                                              src[:, o, ch * CHUNK:(ch + 1) * CHUNK])
                last.then_inc(stats_done[net, layer], 1)
                dve.wait_ge(stats_done[net, layer], 1)

            def scale_of(net, layer, step):
                v = norm[net, layer]
                w = layer_width(net, layer)
                dve.wait_ge(std_ready[net, layer], 1)
                step(nc.vector.reciprocal(v[:, 2, 0:w], v[:, 1, 0:w]))
                nc.vector.tensor_tensor(v[:, 3, 0:w], v[:, 2, 0:w], p_col(net, "g", layer), ALU.mult)
                step(nc.vector.tensor_tensor(v[:, 4, 0:w], v[:, 2, 0:w], v[:, 2, 0:w], ALU.mult))
                step(nc.vector.scalar_tensor_tensor(out=v[:, 5, 0:w], in0=v[:, 4, 0:w], scalar=-0.5,
                                                    in1=v[:, 0, 0:w], op0=ALU.mult, op1=ALU.mult))
                nc.vector.scalar_tensor_tensor(out=v[:, 8, 0:w], in0=v[:, 5, 0:w], scalar=1.5, in1=v[:, 3, 0:w],
                                               op0=ALU.add, op1=ALU.mult).then_inc(scale_ready[net, layer], 1)
                dve.wait_ge(scale_ready[net, layer], 1)

            def aggregate(net, layer, blocks):
                for k in blocks:
                    last = nc.vector.bn_aggr(moments[net, layer][:, k, :],
                                             stats[net, layer][:, k, :, :].rearrange("p a b -> p (a b)"))
                return last

            def coefficients(net, layer, scale_weights=None, blocks=None):
                v = norm[net, layer]
                w = layer_width(net, layer)
                step = chain(bn_step[net, layer], 0)
                step(aggregate(net, layer, range(w) if blocks is None else blocks))
                mean, var = moments[net, layer][:, 0:w, 0], moments[net, layer][:, 0:w, 1]
                step(nc.vector.tensor_scalar_add(v[:, 0, 0:w], var, EPS))
                scale_of(net, layer, step)
                if scale_weights:
                    scale_weights()
                step(nc.vector.tensor_tensor(v[:, 7, 0:w], v[:, 8, 0:w], mean, ALU.mult))
                nc.vector.tensor_tensor(v[:, 9, 0:w], p_col(net, "beta", layer), v[:, 7, 0:w],
                                        ALU.subtract).then_inc(coef_ready[net, layer], 1)

            def layer1(net, blocks=None):
                def scale_w1():
                    for k in range(K0 // 2):
                        nc.vector.tensor_scalar_mul(w1_scaled["hi"][:, k, :], w1_sb[net][:, k, :],
                                                    norm[net, 0][:, 8, k:k + 1]).then_inc(scaled_v[net, 0], 1)
                    for k, hi, count in ((0, scaled_v, 1), (2, scaled_a, 1), (1, scaled_v, 2), (3, scaled_a, 2)):
                        dve.wait_ge(hi[net, 0], count)
                        nc.vector.scalar_tensor_tensor(
                            out=w1_scaled["lo"][:, k, :], in0=w1_sb[net][:, k, :], scalar=norm[net, 0][:, 8, k:k + 1],
                            in1=w1_scaled["hi"][:, k, :], op0=ALU.mult, op1=ALU.subtract).then_inc(w1_lo[net], 1)

                coefficients(net, 0, scale_w1, blocks)
                dve.wait_ge(coef_ready[net, 0], 1)
                step = chain(shift_summed[net], 0)
                shift = norm[net, 0][:, 9, :]
                step(nc.vector.tensor_scalar_mul(shift_w1[:, :], w1_sb[net][:, 0, :], shift[:, 0:1]))
                for k in range(1, K0):
                    step(nc.vector.scalar_tensor_tensor(
                        out=shift_w1[:, :], in0=w1_sb[net][:, k, :], scalar=shift[:, k:k + 1],
                        in1=shift_w1[:, :], op0=ALU.mult, op1=ALU.add))
                dve.wait_ge(fold_done[net, 0], 1)
                nc.vector.tensor_tensor(bias1[net][:, :], small[:, 0:K1], p_col(net, "b", 1),
                                        ALU.add).then_inc(bias_ready[net, 0], 1)
                block_stats(net, 1, [(o, ch) for ch in range(CHUNKS) for o in range(K1)], hidden1)

            def make_rows(step, cols):
                step(nc.vector.tensor_scalar(idx_neg[:, cols], idx_raw[:, cols], 0.0, float(VOCAB),
                                             ALU.is_lt, ALU.mult))
                step(nc.vector.tensor_tensor(idx_wrapped[:, cols], idx_raw[:, cols], idx_neg[:, cols], ALU.add))
                step(nc.vector.tensor_scalar(idx_clamped[:, cols], idx_wrapped[:, cols], 0.0, float(VOCAB - 1),
                                             ALU.max, ALU.min))

            def stage_part(s, cols):
                nc.vector.tensor_tensor(stage[:, s, :], idx_clamped[:, cols], table_base[:, :],
                                        ALU.add).then_inc(slot_open, 1)

            dve.wait_ge(first_idx_loaded, 16)
            step = chain(idx_step, 0)
            make_rows(step, FIRST_COLS)
            dve.wait_ge(base_ready, 2)
            for s in range(SLOTS):
                stage_part(s, slice(s * PW, (s + 1) * PW))
            dve.wait_ge(idx_loaded, 16)
            make_rows(step, LATER_COLS)
            nc.vector.memset(Zs[:, :, :], 0.0).then_inc(cleared, 1)
            nc.vector.memset(idx_clamped[:, PARTS * PW:(PARTS + SLOTS) * PW], 0.0).then_inc(consts_ready, 1)
            nc.vector.memset(idle_operand[:, :], 0.0).then_inc(consts_ready, 1)
            nc.vector.memset(ones[:, :], 1.0).then_inc(consts_ready, 1)
            nc.vector.memset(eps_col[:, :], EPS).then_inc(consts_ready, 1)
            nc.vector.memset(mean_of[:, :], 1.0 / (QUAD * B)).then_inc(consts_ready, 1)
            dve.wait_ge(consts_ready, 5)

            dve.wait_ge(bottom_loaded, 48)
            for n in range(CHUNKS * K0):
                ch, o = divmod(n, K0)
                dve.wait_ge(relu_done["bot", 0], n + 1)
                nc.vector.bn_stats(stats["bot", 0][:, o, ch, :], h0_block[:, n % 2, :])
                dve.wait_ge(h0_hi, n + 1)
                cols = slice(ch * CHUNK, (ch + 1) * CHUNK)
                nc.vector.tensor_tensor(hidden0["lo"][:, o, cols], h0_block[:, n % 2, :],
                                        hidden0["hi"][:, o, cols], ALU.subtract).then_inc(h0_lo["bot"], 1)
            dve.wait_ge(h0_lo["bot"], CHUNKS * K0)
            dve.wait_ge(bw1_loaded, 48)
            layer1("bot")
            coefficients("bot", 1)
            for k in range(K1):
                last = nc.vector.tensor_scalar_mul(w2_scaled[:, k, :], bw2_sb[:, k, :], norm["bot", 1][:, 8, k:k + 1])
            last.then_inc(scaled_v["bot", 1], 1)
            dve.wait_ge(fold_done["bot", 1], 1)
            nc.vector.tensor_tensor(bias2["bot"][:, :], small[:, 0:1], p_col("bot", "b", 2),
                                    ALU.add).then_inc(bias_ready["bot", 1], 1)
            block_stats("bot", 2, [(0, ch) for ch in range(CHUNKS)], x_all[:, :].rearrange("p (a b) -> p a b", a=1))
            coefficients("bot", 2)

            dve.wait_ge(cleared, 1)
            with dve.Fori(0, LOOPS) as it:
                for s in range(SLOTS):
                    i = it * SLOTS + s
                    for g in range(GROUPS):
                        n0, w = 2 * group_pairs(g)[0], 2 * len(group_pairs(g))
                        dve.wait_ge(transposed, i * GROUPS + (g + 1))
                        nc.vector.tensor_copy(
                            TT[:, 0, :, n0:n0 + w].rearrange("p b n -> p n b"),
                            tr_bank[g % 2][:, 0:w * UNIT].rearrange("p (n b) -> p n b", n=w),
                        ).then_inc(tt_written, 1)
                    stage_part(s, bass.ds((i + SLOTS) * PW, PW))
                    for h in range(2):
                        dve.wait_ge(z_done, i * 2 + (h + 1))
                        take_z(nc.vector.tensor_copy, z_bank[h], h, (0, 1)).then_inc(z_taken_v, 1)
                    for o in range(K0):
                        dve.wait_ge(l0_relu, i * K0 + (o + 1))
                        nc.vector.bn_stats(stats["top", 0][:, o, bass.ds(i, 1), :].rearrange("p a b -> p (a b)"),
                                           h0_part[:, o, :]).then_inc(top0_stats, 1)
                        part = bass.ds(i * (2 * UNIT), 2 * UNIT)
                        nc.vector.tensor_tensor(hidden0["lo"][:, o, part], h0_part[:, o, :],
                                                hidden0["hi"][:, o, part], ALU.subtract).then_inc(h0_lo["top"], 1)

            def last_stats(o):
                nc.vector.bn_stats(stats["top", 0][:, o, LAST, :], h0_part[:, o, :]).then_inc(top0_stats, 1)

            def last_lower(h, g):
                dve.wait_ge(last_transposed, h * len(LAST_GROUPS) + g + 1)
                last_tt(nc.vector.tensor_copy, h, g, 0).then_inc(last_tt_v, 1)

            def last_take(h):
                for y in range(2):
                    dve.wait_ge(last_z_done, h * 2 + y + 1)
                    take_z(nc.vector.tensor_copy, z_bank[y], h, (0, 1), y * RX // 2,
                           (y + 1) * RX // 2).then_inc(last_taken_v, 1)

            def last_pre0(h):
                dve.wait_ge(last_l0, h * 2 + 2)
                nc.vector.tensor_copy(pre0[:, h, P:HALF], l0_bank[1][:, 0:P]).then_inc(pre0_v, 1)

            def last_relu(h):
                dve.wait_ge(last_backs, h * 2 + 2)
                for f in range(2):
                    o = 2 * f + 1
                    last = nc.vector.tensor_scalar(h0_part[:, o, h * UNIT:(h + 1) * UNIT],
                                                   l0_bank[3][:, f * UNIT:(f + 1) * UNIT],
                                                   p_col("top", "b", 0)[:, o:o + 1], 0.0, ALU.add, ALU.max)
                last.then_inc(last_relu_v, 1)

            for g in range(len(LAST_GROUPS)):
                last_lower(0, g)
            last_take(0)
            last_lower(1, 0)
            last_pre0(0)
            last_lower(1, 1)
            last_lower(1, 2)
            last_relu(0)
            last_take(1)
            dve.wait_ge(last_relu_a, 2)
            last_stats(0)
            last_stats(2)
            last_pre0(1)
            dve.wait_ge(top0_stats, LAST * K0 + 2)
            aggregate("top", 0, (0, 2))
            last_relu(1)
            dve.wait_ge(last_relu_v, 2)
            last_stats(1)
            last_stats(3)

            dve.wait_ge(top0_stats, PARTS * K0)
            layer1("top", (1, 3))

            def scale_w2():
                for k in range(K1):
                    last = nc.vector.tensor_scalar(tw2_rep[:, k, :], ones[:, 0:QUAD],
                                                   p_col("top", "W", 2)[:, k:k + 1],
                                                   norm["top", 1][:, 8, k:k + 1], ALU.mult, ALU.mult)
                last.then_inc(scaled_v["top", 1], 1)

            coefficients("top", 1, scale_w2)
            dve.wait_ge(coef_ready["top", 1], 1)
            nc.vector.tensor_tensor(shift_w2[:, :], norm["top", 1][:, 9, 0:K1], p_col("top", "W", 2),
                                    ALU.mult).then_inc(scaled_v["top", 1], 1)
            dve.wait_ge(fold_done["top", 1], 1)
            nc.vector.tensor_tensor(bias2["top"][:, :], small[:, 8:9], p_col("top", "b", 2),
                                    ALU.add).then_inc(bias_ready["top", 1], 1)
            dve.wait_ge(mean_done, 1)
            nc.vector.tensor_scalar_mul(neg_mean[:, :], out_bank[1][:, 0:1], -1.0).then_inc(mean_ready, 1)
            dve.wait_ge(sqmean_done, 1)
            v = norm["top", 2]
            dve.wait_ge(std_ready["top", 2], 1)
            nc.vector.tensor_scalar_add(v[:, 0, 0:1], out_bank[2][:, 0:1], EPS).then_inc(bn_step["top", 2], 1)
            scale_of("top", 2, chain(bn_step["top", 2], 1))
            nc.vector.tensor_scalar(v[:, 9, 0:1], neg_mean[:, :], v[:, 8, 0:1], p_col("top", "beta", 2),
                                    ALU.mult, ALU.add).then_inc(coef_ready["top", 2], 1)


def kernel(**inputs):
    import numpy as np
    import concourse.bacc as bacc
    from concourse import mybir as mb
    from concourse.bass_utils import run_bass_kernel_spmd as run

    def get(name):
        return np.ascontiguousarray(inputs[name])

    def columns(vec):
        return vec.reshape(-1, P).T

    dense_t = get("r_dense_inputs").reshape(CHUNKS, UNIT, CU, DENSE).transpose(3, 0, 2, 1).reshape(DENSE, B)
    idx = get("r_sparse_inputs").reshape(CHUNKS, UNIT, CU // 2, 2, TP, 2)
    idx = idx.transpose(5, 1, 0, 2, 4, 3).reshape(P, PARTS * PW)
    params = np.zeros((P, NPARAM), np.float32)
    for (net, what, layer), (at, width) in PARAMS.items():
        vec = get("L0_rec_%s_%s%d" % (net, what, layer)).reshape(-1)
        if vec.size < P:
            vec = np.tile(vec, P // vec.size)
        params[:, at:at + width] = columns(vec)
    w0 = get("L0_rec_top_W0")
    twx = np.zeros((P, H0), np.float32)
    twx[0:D] = w0[0:D]
    tw0x = np.zeros((P, ZC, H0), np.float32)
    for row, (n, m) in enumerate(zip(*np.triu_indices(V, k=1))):
        q, c = divmod(m - 1, ZC)
        tw0x[QUAD * q + n, c] = w0[D + row]

    arrays = {
        "idx": np.ascontiguousarray(idx),
        "table": get("L0_rec_emb_tables").reshape(NF * VOCAB, D),
        "dense_t": np.ascontiguousarray(dense_t),
        "params": params,
        "identity": np.eye(P, dtype=np.float32),
        "bw0": get("L0_rec_bot_W0"), "bw1": get("L0_rec_bot_W1"), "bw2": get("L0_rec_bot_W2"),
        "tw0x": tw0x, "twx": twx, "tw1": get("L0_rec_top_W1"),
    }
    nc = bacc.Bacc("TRN2", target_bir_lowering=False, num_devices=1)
    args = [nc.dram_tensor(k, a.shape, mb.dt.from_np(a.dtype), kind="ExternalInput").ap() for k, a in arrays.items()]
    out = nc.dram_tensor("out", (CHUNKS, CHUNK), mb.dt.float32, kind="ExternalOutput").ap()
    rec_program(nc, *args, out)
    result = run(nc, [arrays], core_ids=[0])
    return result.results[0]["out"].reshape(B, 1)
```
